# Optimizing a Trainium2 kernel written in Bass

```python
import numpy as np
import jax
import jax.numpy as jnp

def _softmax(x, axis=-1):
    return jax.nn.softmax(x, axis=axis)

def _gelu(x):
    return jax.nn.gelu(x, approximate=True)

def _silu(x):
    return jax.nn.silu(x)

def _sigmoid(x):
    return jax.nn.sigmoid(x)

def _layernorm(x, axis=-1, eps=1e-05):
    m = jnp.mean(x, axis=axis, keepdims=True)
    v = jnp.var(x, axis=axis, keepdims=True)
    return (x - m) / jnp.sqrt(v + eps)

def _scatter_add(tgt, idx, src, axis=0):
    return tgt.at[idx].add(src)

def _segment_sum(src, seg, n):
    return jax.ops.segment_sum(src, seg, n)
kernel_name = 'mk_adaln_d1_jaxref_r8_dedfb1'

def setup_inputs(seed: int=0):
    np.random.seed(seed)
    _w = jnp.asarray

    def _L0_attn_setup():
        import jax, jax.numpy as jnp
        import numpy as np
        E = 256
        H = 16
        HD = E // H
        CKV = 64
        CQ = 192
        RD = 64
        SCALE = 1.0 / np.sqrt(HD + RD)

        def _rope(qr, kr, offset=0):
            s = qr.shape[2]
            t = jnp.arange(offset, offset + s, dtype=jnp.float32)
            inv_freq = 1.0 / 10000.0 ** (jnp.arange(0, RD, 2, dtype=jnp.float32) / RD)
            freqs = t[:, None] * inv_freq[None, :]
            cos = jnp.concatenate([jnp.cos(freqs)] * 2, axis=-1)
            sin = jnp.concatenate([jnp.sin(freqs)] * 2, axis=-1)

            def rot(x):
                x1, x2 = (x[..., :RD // 2], x[..., RD // 2:])
                return jnp.concatenate([-x2, x1], axis=-1)
            return (qr * cos + rot(qr) * sin, kr * cos + rot(kr) * sin)
        key = jax.random.key(seed)
        ks = jax.random.split(key, 10)

        def w(k, out_d, in_d):
            return jax.random.normal(k, (out_d, in_d), jnp.float32) * (1.0 / np.sqrt(in_d))
        return {'x': jax.random.normal(ks[0], (2, 256, E), jnp.float32), 'w_dq': w(ks[1], CQ, E), 'w_uq': w(ks[2], H * HD, CQ), 'w_dkv': w(ks[3], CKV, E), 'w_uk': w(ks[4], H * HD, CKV), 'w_uv': w(ks[5], H * HD, CKV), 'w_qr': w(ks[6], H * RD, CQ), 'w_kr': w(ks[7], H * RD, E), 'w_out': w(ks[8], E, E)}
    _L0_attn_in = _L0_attn_setup()

    def _L0_ffn_setup():
        import jax, jax.numpy as jnp
        import numpy as np
        TOP_K = 8
        NUM_GROUPS = 8
        key = jax.random.key(seed)
        ks = jax.random.split(key, 6)
        T_B, T_S, H, I, E, G = (1, 256, 256, 96, 32, NUM_GROUPS)
        hidden_states = jax.random.normal(ks[0], (T_B, T_S, H), dtype=jnp.float32)
        gate_weight = jax.random.normal(ks[1], (E, H), dtype=jnp.float32) * 0.02
        gate_up_proj = jax.random.normal(ks[2], (E, 2 * I, H), dtype=jnp.float32) * 0.02
        down_proj = jax.random.normal(ks[3], (E, H, I), dtype=jnp.float32) * 0.02
        merge_groups = jax.random.randint(ks[4], (E,), 0, G, dtype=jnp.int64)
        merge_groups = merge_groups.at[:G].set(jnp.arange(G, dtype=jnp.int64))
        dominant_experts = jax.random.randint(ks[5], (G,), 0, E, dtype=jnp.int64)
        return {'hidden_states': hidden_states, 'gate_weight': gate_weight, 'gate_up_proj': gate_up_proj, 'down_proj': down_proj, 'merge_groups': merge_groups, 'dominant_experts': dominant_experts}
    _L0_ffn_in = _L0_ffn_setup()
    _L0_c = _w((lambda *s: np.random.randn(*s).astype(np.float32) * 0.05)(8, 256))
    _L0_wmod = _w((lambda *s: np.random.randn(*s).astype(np.float32) * 0.05)(256, 6 * 256) * 256 ** (-0.5))
    _d = {'L0_attn_x': _L0_attn_in['x'], 'L0_attn_w_dq': _L0_attn_in['w_dq'], 'L0_attn_w_uq': _L0_attn_in['w_uq'], 'L0_attn_w_dkv': _L0_attn_in['w_dkv'], 'L0_attn_w_uk': _L0_attn_in['w_uk'], 'L0_attn_w_uv': _L0_attn_in['w_uv'], 'L0_attn_w_qr': _L0_attn_in['w_qr'], 'L0_attn_w_kr': _L0_attn_in['w_kr'], 'L0_attn_w_out': _L0_attn_in['w_out'], 'L0_ffn_gate_weight': _L0_ffn_in['gate_weight'], 'L0_ffn_gate_up_proj': _L0_ffn_in['gate_up_proj'], 'L0_ffn_down_proj': _L0_ffn_in['down_proj'], 'L0_ffn_merge_groups': _L0_ffn_in['merge_groups'], 'L0_ffn_dominant_experts': _L0_ffn_in['dominant_experts'], 'L0_c': _L0_c, 'L0_wmod': _L0_wmod}
    _x0 = _d['L0_attn_x']
    _d['L0_attn_x'] = jax.random.normal(jax.random.fold_in(jax.random.key(seed), 1), (8, 512, 256), dtype=_x0.dtype)
    del _x0
    return _d

def reference(L0_attn_x, L0_attn_w_dq, L0_attn_w_uq, L0_attn_w_dkv, L0_attn_w_uk, L0_attn_w_uv, L0_attn_w_qr, L0_attn_w_kr, L0_attn_w_out, L0_ffn_gate_weight, L0_ffn_gate_up_proj, L0_ffn_down_proj, L0_ffn_merge_groups, L0_ffn_dominant_experts, L0_c, L0_wmod):

    def _L0_attn_ref(x, w_dq, w_uq, w_dkv, w_uk, w_uv, w_qr, w_kr, w_out):
        import jax, jax.numpy as jnp
        import numpy as np
        E = 256
        H = 16
        HD = E // H
        CKV = 64
        CQ = 192
        RD = 64
        SCALE = 1.0 / np.sqrt(HD + RD)

        def _rope(qr, kr, offset=0):
            s = qr.shape[2]
            t = jnp.arange(offset, offset + s, dtype=jnp.float32)
            inv_freq = 1.0 / 10000.0 ** (jnp.arange(0, RD, 2, dtype=jnp.float32) / RD)
            freqs = t[:, None] * inv_freq[None, :]
            cos = jnp.concatenate([jnp.cos(freqs)] * 2, axis=-1)
            sin = jnp.concatenate([jnp.sin(freqs)] * 2, axis=-1)

            def rot(x):
                x1, x2 = (x[..., :RD // 2], x[..., RD // 2:])
                return jnp.concatenate([-x2, x1], axis=-1)
            return (qr * cos + rot(qr) * sin, kr * cos + rot(kr) * sin)
        b, s, _ = x.shape
        c_q = x @ w_dq.T
        q_c = (c_q @ w_uq.T).reshape(b, s, H, HD).transpose(0, 2, 1, 3)
        c_kv = x @ w_dkv.T
        k_c = (c_kv @ w_uk.T).reshape(b, s, H, HD).transpose(0, 2, 1, 3)
        v = (c_kv @ w_uv.T).reshape(b, s, H, HD).transpose(0, 2, 1, 3)
        q_r = (c_q @ w_qr.T).reshape(b, s, H, RD).transpose(0, 2, 1, 3)
        k_r = (x @ w_kr.T).reshape(b, s, H, RD).transpose(0, 2, 1, 3)
        q_r, k_r = _rope(q_r, k_r, offset=0)
        q = jnp.concatenate([q_c, q_r], axis=-1)
        k = jnp.concatenate([k_c, k_r], axis=-1)
        attn = jnp.einsum('bhqd,bhkd->bhqk', q, k) * SCALE
        mask = jnp.triu(jnp.full((s, s), -jnp.inf, jnp.float32), k=1)
        attn = jax.nn.softmax((attn + mask).astype(jnp.float32), axis=-1).astype(q.dtype)
        out = jnp.einsum('bhqk,bhkd->bhqd', attn, v)
        out = out.transpose(0, 2, 1, 3).reshape(b, s, H * HD)
        return out @ w_out.T

    def _L0_ffn_ref(hidden_states, gate_weight, gate_up_proj, down_proj, merge_groups, dominant_experts):
        import jax, jax.numpy as jnp
        import numpy as np
        TOP_K = 8
        NUM_GROUPS = 8
        B, S, H = hidden_states.shape
        G = dominant_experts.shape[0]
        x = hidden_states.reshape(-1, H)
        logits = jnp.einsum('th,eh->te', x, gate_weight)
        probs = jax.nn.softmax(logits.astype(jnp.float32), axis=-1).astype(logits.dtype)
        top_val, top_idx = jax.lax.top_k(probs, TOP_K)
        top_val = top_val / jnp.sum(top_val, axis=-1, keepdims=True)
        sel_group = merge_groups[top_idx]
        onehot = jax.nn.one_hot(sel_group, G, dtype=top_val.dtype)
        w_tg = jnp.einsum('tk,tkg->tg', top_val, onehot)
        gu = gate_up_proj[dominant_experts]
        dn = down_proj[dominant_experts]
        h = jnp.einsum('th,goh->tgo', x, gu)
        gate, up = jnp.split(h, 2, axis=-1)
        act = jax.nn.silu(gate) * up
        y = jnp.einsum('tgi,ghi->tgh', act, dn)
        out = jnp.einsum('tg,tgh->th', w_tg, y)
        return out.reshape(B, S, H)
    x = L0_attn_x
    mod = (_silu(L0_c) @ L0_wmod).reshape(L0_c.shape[0], 6, 1, -1)
    sa, ca, ga, sb, cb, gb = (mod[:, 0], mod[:, 1], mod[:, 2], mod[:, 3], mod[:, 4], mod[:, 5])
    ga = (2 * (ga >= 0) - 1) * jnp.maximum(jnp.abs(ga), 0.25)
    gb = (2 * (gb >= 0) - 1) * jnp.maximum(jnp.abs(gb), 0.25)
    h = _layernorm(x, axis=-1) * (1 + ca) + sa
    x = x + ga * _L0_attn_ref(h, L0_attn_w_dq, L0_attn_w_uq, L0_attn_w_dkv, L0_attn_w_uk, L0_attn_w_uv, L0_attn_w_qr, L0_attn_w_kr, L0_attn_w_out)
    h = _layernorm(x, axis=-1) * (1 + cb) + sb
    x = x + gb * _L0_ffn_ref(h, L0_ffn_gate_weight, L0_ffn_gate_up_proj, L0_ffn_down_proj, L0_ffn_merge_groups, L0_ffn_dominant_experts)
    return x

_drawn_inputs = setup_inputs


def setup_inputs(seed=0):
    import zlib

    import numpy as np

    out = dict(_drawn_inputs(seed))
    spreads = {}
    factors = {'L0_ffn_gate_weight': 8.0, 'L0_ffn_gate_up_proj': 8.0, 'L0_ffn_down_proj': 8.0}
    for name, (base, spread) in spreads.items():
        noise = np.random.default_rng([zlib.crc32(name.encode()), seed]).standard_normal(out[name].shape)
        drawn = base * np.exp(spread * noise) if base else spread * noise
        out[name] = jnp.asarray(drawn.astype(out[name].dtype))
    for name, factor in factors.items():
        out[name] = (out[name] * factor).astype(out[name].dtype)
    return out
```

```python
from contextlib import ExitStack

import numpy as np

import concourse.bass as bass
from concourse import mybir

ALU = mybir.AluOpType
ACT = mybir.ActivationFunctionType
AX_X = mybir.AxisListType.X
F32 = mybir.dt.float32
F32R = mybir.dt.float32r
BF16 = mybir.dt.bfloat16
I32 = mybir.dt.int32

P = 128
B, S, E = 8, 512, 256
H, HD, RD = 16, 16, 64
HALF = RD // 2
CQ, CKV = 192, 64
HG = 4
NG = H // HG
DK = RD + HD
TT = S // P
EC = E // P
SCALE = float(1.0 / np.sqrt(DK))
EPS = 1e-5
NX, TOPK, G, FI = 32, 8, 8, 96
FT = G * FI // P
NROPE = 2 * P
NQ = NG * NROPE + H * HD
MASKED = -1.0e30

PT_N = [S - j * P for j in range(TT)]
PT_OFF = [(j % 2) * HG * PT_N[0] for j in range(TT)]
PT_COLS = HG * (PT_N[0] + PT_N[1])
ST_JOBS = [(0, 0, 1), (0, 1, 1), (0, 2, 1), (0, 3, 1), (1, 0, 1), (1, 1, 1), (1, 2, 1), (1, 3, 1),
           (2, 0, 2), (2, 2, 2), (3, 0, 4)]
NST = len(ST_JOBS)
MAX_JOBS = []
for _h in (0, 2):
    MAX_JOBS += [[(_h, 3)], [(_h, 0), (_h, 2)], [(_h + 1, 3)], [(_h + 1, 0), (_h + 1, 2)], [(_h, 1), (_h + 1, 1)]]
NMAX = len(MAX_JOBS)
MAX_FROM = 5
FULL_RING, PROB_RING, OT_BANKS = 4, 2, 2
FUSE = [(c, at, min(512, NQ - at)) for c in range(EC) for at in range(0, NQ, 512)]


def project_steps(ahead, g, between=()):
    out = [("rope", ahead, g, 0), ("rotate", ahead, g, 0), *between, ("rope", ahead, g, 1), ("rotate", ahead, g, 1)]
    if g % 2 == 0:
        out.append(("content", ahead, g))
    return out + [("heads", ahead, g)]


def attend_steps(g, maxima):
    out, at = [], 0
    for n in range(NST):
        out.append(("score", 0, g, n))
        if n in (7, 9, 10):
            out.append(("value", 0, g, ST_JOBS[n][0] - 1))
        if n >= MAX_FROM:
            take = (len(maxima) * (n - MAX_FROM + 1)) // (NST - MAX_FROM)
            out += maxima[at:take]
            at = take
    return out + [("value", 0, g, TT - 1)]


def all_maxima(ahead, g):
    return [("maxima", ahead, g, i) for i in range(NMAX)]


def setup_steps():
    out = [("stats1", 0), ("mod",), ("gates",), ("norm1", 0), ("turn1", 0, 0), ("turn1", 0, 1)]
    out += [("fuse", i) for i in range(len(FUSE))]
    out += [("latent", 0)] + project_steps(0, 0) + [("values", 0, 0), ("values", 0, 1)]
    return out + all_maxima(0, 0) + project_steps(0, 1) + [("shift", 0, 0), ("split_ffn",)]


def body_steps(last):
    def next_batch(*steps):
        return [] if last else list(steps)

    out = [("loads", 0)] + next_batch(("load_next", 1)) + attend_steps(0, all_maxima(0, 1))
    out += project_steps(0, 2, [("shift", 0, 1)]) + [("attn_out", 0, 0)]
    out += next_batch(("stats1", 1)) + attend_steps(1, all_maxima(0, 2))
    out += project_steps(0, 3, [("shift", 0, 2)]) + [("attn_out", 0, 1)]
    out += next_batch(("norm1", 1)) + attend_steps(2, all_maxima(0, 3))
    out += next_batch(("turn1", 1, 0), ("turn1", 1, 1)) + [("shift", 0, 3)]
    out += next_batch(("latent", 1), *project_steps(1, 0)) + [("attn_out", 0, 2)]
    out += attend_steps(3, next_batch(*all_maxima(1, 0))) + [("attn_out", 0, 3)]
    out += next_batch(("values", 1, 0), ("values", 1, 1), ("rope", 1, 1, 0), ("rotate", 1, 1, 0))
    out += [("mix", 0, 0), ("mix", 0, 1), ("stats2", 0), ("norm2", 0)]
    out += next_batch(("shift", 1, 0), ("rope", 1, 1, 1))
    out += [("turn2", 0, 0), ("turn2", 0, 1)] + next_batch(("rotate", 1, 1, 1), ("heads", 1, 1))
    out += [("logits", 0, 0), ("logits", 0, 1), ("top", 0)]
    out += [("gate", 0, 0), ("up", 0, 0), ("gate", 0, 1), ("up", 0, 1), ("turn_w", 0), ("gate", 0, 2), ("up", 0, 2)]
    for k in range(3, FT):
        out += [("weigh", 0, k - 3), ("gate", 0, k), ("up", 0, k)]
    return out + [("weigh", 0, k) for k in range(FT - 3, FT)] + [("down", 0, 0), ("down", 0, 1), ("store", 0)]


def banks_of(step):
    kind = step[0]
    if kind in ("rope", "content"):
        return 2
    return int(kind in ("mod", "gates", "turn1", "turn2", "fuse", "latent", "values", "maxima", "shift", "mix",
                        "logits", "gate", "up", "turn_w", "weigh", "down"))


def ring_places(steps):
    place, n = {}, 0
    for s in steps:
        for i in range(banks_of(s)):
            place[(*s, i) if banks_of(s) > 1 else s] = n
            n += 1
    return place, n


SETUP, FIRST, LAST = setup_steps(), body_steps(False), body_steps(True)
PLACES = {}
for _name, _steps in (("setup", SETUP), ("body", FIRST), ("last", LAST)):
    PLACES[_name] = ring_places(_steps)
NSETUP, NBODY = PLACES["setup"][1], PLACES["body"][1]
assert NBODY % FULL_RING == 0


class Count:

    def __init__(self, sem, per, by=1):
        self.sem, self.per, self.by = sem, per, by

    def at(self, b, ahead, k):
        return b * (self.per * self.by) + (ahead * self.per + k + 1) * self.by


def block_program(nc, x, wu_t, w_dq, wk_t, wdkv_t, wuk_t, wuv_t, wo_p, gw_t, gup_t, dn_t, groups, chosen,
                  c_t, wmod, cos_t, sin_t, out):
    gates_dram = nc.dram_tensor("gates_scratch", [B, 2 * E], F32, kind="Internal").ap()
    ctx = ExitStack()
    with ctx:
        def sb(name, shape, dt=F32):
            return ctx.enter_context(nc.sbuf_tensor(name, shape, dt))

        def sem(name):
            return ctx.enter_context(nc.semaphore(name))

        wq_hi, wq_lo = sb("wq_hi", [P, EC, NQ], F32R), sb("wq_lo", [P, EC, NQ], F32R)
        wk_hi, wk_lo = sb("wk_hi", [P, EC, NG * NROPE], F32R), sb("wk_lo", [P, EC, NG * NROPE], F32R)
        wd_hi, wd_lo = sb("wd_hi", [P, EC, CKV], F32R), sb("wd_lo", [P, EC, CKV], F32R)
        gu_hi, gu_lo = sb("gu_hi", [P, EC, 2 * G * FI], F32R), sb("gu_lo", [P, EC, 2 * G * FI], F32R)
        gw_hi, gw_lo = sb("gw_hi", [P, EC, NX], F32R), sb("gw_lo", [P, EC, NX], F32R)
        wuk, wuv = sb("wuk", [CKV, E]), sb("wuv", [CKV, E])
        wo = sb("wo", [P, NG, E])
        dn = sb("dn", [P, FT, E])
        spread = sb("spread", [2 * NX, G * FI], F32R)
        cos_sb, sin_sb = sb("cos_sb", [P, S]), sb("sin_sb", [P, S])
        modT = sb("modT", [P, 8, B])
        gate_bc = sb("gate_bc", [P, 2 * E])
        ident, ident_b = sb("ident", [P, P]), sb("ident_b", [P, P], BF16)
        mask_qk, mask_kq = sb("mask_qk", [P, P], BF16), sb("mask_kq", [P, P], BF16)
        half_neg = sb("half_neg", [P, TT])
        xn = sb("xn", [P, TT, E])
        xr = sb("xr", [P, TT, E])
        hf = sb("hf", [P, EC, S])
        h1_hi, h1_lo = sb("h1_hi", [P, EC, S], F32R), sb("h1_lo", [P, EC, S], F32R)
        h2_hi, h2_lo = sb("h2_hi", [P, EC, S], F32R), sb("h2_lo", [P, EC, S], F32R)
        ckv = sb("ckv", [CKV, S])
        vals = sb("vals", [P, TT, H, 2 * HD])
        rot = sb("rot", [P, 2, 4, S])
        con = sb("con", [P, 2, S])
        qh = sb("qh", [P, 2, HG, S], F32R)
        kh = sb("kh", [P, 2, HG, S], F32R)
        pt = sb("pt", [P, PT_COLS])
        act = pt[:, 0:FT * S].rearrange("p (k s) -> p k s", k=FT)
        on = sb("on", [P, NG, S])
        small = sb("small", [P, 256])
        norm_bc, norm_r = sb("norm_bc", [P, S])[:, :], sb("norm_r", [P, S])[:, :]
        sum2 = hf[:, 0, :].rearrange("p (t e) -> p t e", t=2)
        th = on[:, 0:2, :]
        wT = sb("wT", [2 * NX, S], F32R)
        mcol = sb("mcol", [P, 2, HG * TT])
        nm = sb("nm", [HG * TT, 2, P])
        stat, mv = small[:, 0:24].rearrange("p (t k) -> p t k", t=TT), small[:, 24:32].rearrange("p (t k) -> p t k", t=TT)
        veps, rstd = small[:, 32:36], small[:, 36:40]
        lg = sb("lg", [P, TT, NX])
        ex = sb("ex", [P, TT, NX])
        rest = sb("rest", [P, TT, NX])
        top8 = small[:, 40:72].rearrange("p (t k) -> p t k", t=TT)
        mx, den, rden = small[:, 72:76], small[:, 76:80], small[:, 80:84]
        scT = sb("scT", [P, EC, B])
        ct = sb("ct", [P, EC, B])
        gid = small[0:2 * NX, 100:101]
        idx_sb = sb("idx_sb", [1, G], I32)
        grp_i = sb("grp_i", [2 * NX, 1], I32)
        gclamp = rot[0:B, 1, 2:4, :]
        wmod_st = pt[:, 0:EC * 6 * E].rearrange("p (c n) -> p c n", c=EC)
        wk_st = on[:, :, :].rearrange("p g s -> p (g s)").rearrange("p (c n) -> p c n", c=EC)
        gu_st = pt[:, 0:EC * 2 * G * FI].rearrange("p (c n) -> p c n", c=EC)
        rot_flat = rot[:, :, :, :].rearrange("p a b s -> p (a b s)")
        wu_st = rot_flat[:, 0:2 * NQ].rearrange("p (c n) -> p c n", c=2)
        wdq_st = rot_flat[:, 2 * NQ:2 * NQ + 2 * E].rearrange("p (c n) -> p c n", c=2)
        wd_st = rot_flat[:, 3200:3200 + EC * CKV].rearrange("p (c n) -> p c n", c=EC)
        gw_st = rot_flat[:, 3400:3400 + EC * NX].rearrange("p (c n) -> p c n", c=EC)
        gnum = hf[:, :, :].rearrange("p a s -> p (a s)")[:, 0:G * FI]

        full = [ctx.enter_context(nc.psum_tensor(f"full{i}", [P, 512], F32)) for i in range(FULL_RING)]
        prob = [ctx.enter_context(nc.psum_tensor(f"prob{i}", [P, 512], F32)) for i in range(PROB_RING)]
        ot = [ctx.enter_context(nc.psum_tensor(f"ot{i}", [P, 512], F32)) for i in range(OT_BANKS)]

        ld_x, ld_mod, ld_q, ld_k, ld_tab, ld_small, ld_ffn, ld_idx = (
            sem(n) for n in ("ld_x", "ld_mod", "ld_q", "ld_k", "ld_tab", "ld_small", "ld_ffn", "ld_idx"))
        x_loaded = Count(sem("x_loaded"), 1, 16)
        res_loaded = Count(sem("res_loaded"), 1, 16)
        gate_loaded = Count(sem("gate_loaded"), 1, 16)
        gates_stored = sem("gates_stored")
        stored = Count(sem("stored"), 1, 16)
        NHD = 6
        heads_loaded = [Count(sem(f"heads_loaded{i}"), NG // 2, 16 * NHD) for i in range(2)]
        shift_loaded = [Count(sem(f"shift_loaded{i}"), NG // 2, 16 * HG) for i in range(2)]
        full_sem, prob_sem = sem("full_filled"), sem("prob_filled")
        prob_filled = Count(prob_sem, NG * NST)
        value_added = Count(sem("value_added"), NG * TT)
        stats_read = [Count(sem(f"stats{i}_read"), 1) for i in (1, 2)]
        aggregated = [Count(sem(f"aggregated{i}"), 1) for i in (1, 2)]
        var_ready = [Count(sem(f"var{i}_ready"), 1) for i in (1, 2)]
        normed = [Count(sem(f"normed{i}"), 1) for i in (1, 2)]
        hi_ready = [Count(sem(f"h{i}_hi_ready"), EC) for i in (1, 2)]
        lo_ready = [Count(sem(f"h{i}_lo_ready"), EC) for i in (1, 2)]
        rotated = Count(sem("rotated"), 2 * NG)
        max_read = Count(sem("max_read"), NG * NMAX)
        sums_moved = Count(sem("sums_moved"), NG)
        sums_inverted = Count(sem("sums_inverted"), NG)
        attn_ready = Count(sem("attn_ready"), NG)
        mix_gated = Count(sem("mix_gated"), 2)
        mix_added = Count(sem("mix_added"), 2)
        logits_read = Count(sem("logits_read"), 2)
        row_max = Count(sem("row_max"), 1)
        logits_shifted = Count(sem("logits_shifted"), 1)
        top_found = Count(sem("top_found"), 1)
        top_removed = Count(sem("top_removed"), 1)
        top_summed = Count(sem("top_summed"), 1)
        sum_inverted = Count(sem("sum_inverted"), 1)
        top_kept = Count(sem("top_kept"), 1)
        weights_ready = Count(sem("weights_ready"), 1)
        wT_lo_ready = Count(sem("wT_lo_ready"), 1)
        gate_used = Count(sem("gate_used"), FT)
        up_used = Count(sem("up_used"), FT)
        inner_ready = Count(sem("inner_ready"), FT)
        down_gated = Count(sem("down_gated"), 2)
        down_added = Count(sem("down_added"), 2)
        dve_setup = sem("dve_setup")
        keys_split, key_ones = sem("keys_split"), sem("key_ones")
        waits_passed = sem("waits_passed")
        setup_chain = sem("setup_chain")
        rstd_ready = [Count(sem(f"rstd{i}_ready"), 1) for i in (1, 2)]
        rope_ready = Count(sem("rope_ready"), 2 * NG)
        consts_ready, pool_setup = sem("consts_ready"), sem("pool_setup")
        turned = [Count(sem(f"h{i}_modulated"), EC) for i in (1, 2)]
        latent_ready = Count(sem("latent_ready"), 1)
        vals_ready = Count(sem("vals_ready"), 2)
        con_ready = Count(sem("con_ready"), NG)
        nm_ready = Count(sem("nm_ready"), NG)
        exp_ready = Count(sem("exp_ready"), NG * NST)
        top_exp = Count(sem("top_exp"), 1)
        wT_hi_ready = Count(sem("wT_hi_ready"), 1)
        tanh_ready = Count(sem("tanh_ready"), FT)
        act_setup = sem("act_setup")

        def full_value(b, part, place):
            if part == "setup":
                return place + 1
            return b * NBODY + (NSETUP + place + 1)

        def bank(part, place):
            return full[(place if part == "setup" else NSETUP + place) % FULL_RING]

        def wait_full(e, b, part, step):
            place = PLACES[part][0][step]
            e.wait_ge(full_sem, full_value(b, part, place))
            return bank(part, place)

        def wait(e, count, b, ahead, k):
            v = count.at(b, ahead, k)
            if not isinstance(v, int) or v > 0:
                e.wait_ge(count.sem, v)

        def wait_alone(e, count, b, ahead, k):
            wait(e, count, b, ahead, k)
            e.sem_inc(waits_passed, 1)

        def reader(step):
            kind, ahead = step[0], step[1] if len(step) > 1 else 0
            return {
                "turn1": lambda: (turned[0], ahead, step[2]),
                "turn2": lambda: (turned[1], ahead, step[2]),
                "latent": lambda: (latent_ready, ahead, 0),
                "values": lambda: (vals_ready, ahead, step[2]),
                "rope": lambda: (rotated, ahead, 2 * step[2] + step[3]),
                "content": lambda: (con_ready, ahead, step[2] + step[3]),
                "maxima": lambda: (max_read, ahead, NMAX * step[2] + step[3]),
                "shift": lambda: (nm_ready, ahead, step[2]),
                "mix": lambda: (mix_gated, ahead, step[2]),
                "logits": lambda: (logits_read, ahead, step[2]),
                "gate": lambda: (gate_used, ahead, step[2]),
                "up": lambda: (up_used, ahead, step[2]),
                "turn_w": lambda: (wT_lo_ready, ahead, 0),
                "weigh": lambda: (inner_ready, ahead, step[2]),
                "down": lambda: (down_gated, ahead, step[2]),
            }[kind]()

        ORDER = {part: sorted(PLACES[part][0], key=PLACES[part][0].get) for part in PLACES}
        SETUP_READ = {("mod",): 2, ("gates",): 4, **{("fuse", i): 6 + i for i in range(6)}}

        def take_bank(e, b, part, step):
            place = PLACES[part][0][step]
            back = place - FULL_RING
            if back >= 0:
                prev, shift = ORDER[part][back], 0
            elif part == "setup":
                prev = None
            elif isinstance(b, int) and b == 0:
                prev, shift = ORDER["setup"][back], 0
            else:
                prev, shift = ORDER["body"][back], -1
            if prev is not None:
                if prev in SETUP_READ:
                    e.wait_ge(dve_setup, SETUP_READ[prev])
                else:
                    count, ahead, k = reader(prev)
                    wait(e, count, b, ahead + shift, k)
            return bank(part, place)

        def parts(program):
            def run(e):
                program(e, 0, "setup", SETUP)
                program(e, 0, "body", FIRST)
                with e.Fori(1, B - 1) as b:
                    program(e, b, "body", FIRST)
                program(e, B - 1, "last", LAST)
            return run

        def head_value(b, ahead, g):
            ahead, g = ahead + g // NG, g % NG
            return g % 2, ahead, g // 2

        def wait_parity(e, counts, b, ahead, g):
            par, ahead, k = head_value(b, ahead, g)
            wait(e, counts[par], b, ahead, k)

        block = ctx.enter_context(nc.Block())

        @block.sync
        def _(sp):
            def x_rows(b, ahead):
                return x[bass.ds(b + ahead, 1), :, :].rearrange("o (t p) e -> p (o t) e", p=P)

            sp.dma_start(xn[:, :, :], x_rows(0, 0)).then_inc(x_loaded.sem, 16)
            sp.dma_start(ct[:, :, :], c_t.rearrange("(c p) b -> p c b", p=P)).then_inc(ld_mod, 16)
            sp.dma_start(wmod_st, wmod.rearrange("(c p) n -> p c n", p=P)).then_inc(ld_mod, 16)
            sp.dma_start(wu_st[:, 0, :], wu_t[0:P, :]).then_inc(ld_q, 16)
            sp.dma_start(wu_st[0:CQ - P, 1, :], wu_t[P:CQ, :]).then_inc(ld_q, 16)
            sp.dma_start(wdq_st[:, 0, :], w_dq[0:P, :]).then_inc(ld_q, 16)
            sp.dma_start(wdq_st[0:CQ - P, 1, :], w_dq[P:CQ, :]).then_inc(ld_q, 16)
            sp.dma_start(wk_st, wk_t.rearrange("(c p) n -> p c n", p=P)).then_inc(ld_k, 16)
            sp.dma_start(wd_st, wdkv_t.rearrange("(c p) n -> p c n", p=P)).then_inc(ld_k, 16)
            sp.dma_start(gw_st, gw_t.rearrange("(c p) n -> p c n", p=P)).then_inc(ld_k, 16)
            sp.dma_start(cos_sb[:, :], cos_t).then_inc(ld_tab, 16)
            sp.dma_start(sin_sb[:, :], sin_t).then_inc(ld_tab, 16)
            sp.dma_start(wuk[:, :], wuk_t).then_inc(ld_small, 16)
            sp.dma_start(wuv[:, :], wuv_t).then_inc(ld_small, 16)
            sp.dma_start(wo[:, :, :], wo_p.rearrange("g p e -> p g e")).then_inc(ld_small, 16)
            sp.dma_start(grp_i[0:NX, :], groups).then_inc(ld_small, 16)
            sp.dma_start(grp_i[NX:2 * NX, :], groups).then_inc(ld_small, 16)
            sp.dma_start(idx_sb[:, :], chosen).then_inc(ld_idx, 16)
            sp.wait_ge(ld_idx, 16)
            sp.wait_ge(dve_setup, 4)
            sp.dma_start(gates_dram, gclamp[:, 0, :]).then_inc(gates_stored, 16)
            for g in range(G):
                xp = sp.value_load(idx_sb[0:1, g:g + 1], min_val=0, max_val=NX - 1)
                src = gup_t[bass.ds(xp, 1), :, :].rearrange("o (c p) n -> p (o c) n", p=P)
                for half in range(2):
                    at = half * G * FI + g * FI
                    sp.dma_start(gu_st[:, :, at:at + FI], src[:, :, half * FI:(half + 1) * FI]).then_inc(ld_ffn, 16)
                for r in range(0, FI, 32):
                    row = g * FI + r
                    sp.dma_start(dn[row % P:row % P + 32, row // P, :],
                                 dn_t[bass.ds(xp, 1), r:r + 32, :].rearrange("o r e -> (o r) e")).then_inc(ld_ffn, 16)
            sp.wait_ge(gates_stored, 16)
            sp.wait_ge(key_ones, 1)

            def program(sp, b, part, steps):
                for step in steps:
                    kind, ahead = step[0], step[1] if len(step) > 1 else 0
                    if kind == "heads":
                        g = step[2]
                        par, head_ahead, k = head_value(b, ahead, g)
                        wait_alone(sp, prob_filled, b, ahead, (g - 2) * NST + NST - 1)
                        for t, dst in ((0, kh), (1, qh)):
                            wait_alone(sp, rope_ready, b, ahead, 2 * g + t)
                            wait_alone(sp, con_ready, b, ahead, 2 * (g // 2) + t)
                            for half, slot in ((0, 0), (1, 3)):
                                sp.dma_start(dst[half * HALF:(half + 1) * HALF, par, :, :].bitcast(F32),
                                             rot[:, t, slot, :]).then_inc(heads_loaded[par].sem, 16)
                            row = (g % 2) * HG * HD
                            sp.dma_start(dst[RD:DK, par, :, :].bitcast(F32), con[row:row + HG * HD, t, :])\
                              .then_inc(heads_loaded[par].sem, 16)
                    elif kind == "shift":
                        g = step[2]
                        wait_alone(sp, nm_ready, b, ahead, g)
                        for h in range(HG):
                            sp.dma_start(qh[DK:DK + 1, g % 2, h, :].bitcast(F32).rearrange("o (q t) -> o q t", q=TT),
                                         nm[h * TT:(h + 1) * TT, g % 2, :]).then_inc(shift_loaded[g % 2].sem, 16)
                    elif kind == "loads":
                        wait_alone(sp, stored, b, ahead - 1, 0)
                        wait_alone(sp, down_gated, b, ahead - 1, 1)
                        sp.dma_start(xr[:, :, :], x_rows(b, ahead)).then_inc(res_loaded.sem, 16)
                        sp.dma_start(gate_bc[:, :], gates_dram[bass.ds(b + ahead, 1), :].broadcast_to([P, 2 * E]))\
                          .then_inc(gate_loaded.sem, 16)
                    elif kind == "load_next":
                        if isinstance(b, int) and b == 0:
                            sp.wait_ge(full_sem, full_value(0, "setup", PLACES["setup"][0][("turn1", 0, 1)]))
                        else:
                            sp.wait_ge(full_sem, full_value(b, "body", PLACES["body"][0][("turn2", 0, 1)] - NBODY))
                            sp.sem_inc(waits_passed, 1)
                        sp.dma_start(xn[:, :, :], x_rows(b, ahead)).then_inc(x_loaded.sem, 16)
                    elif kind == "store":
                        wait_alone(sp, down_added, b, ahead, 1)
                        sp.dma_start(out[bass.ds(b + ahead, 1), :, :].rearrange("o (t p) e -> p (o t) e", p=P),
                                     xr[:, :, :]).then_inc(stored.sem, 16)
            parts(program)(sp)
            sp.wait_ge(stored.sem, 16 * B)

        @block.gpsimd
        def _(pool):
            pool.memset(ident[:, :], 0.0).then_inc(pool_setup, 1)
            pool.memset(mask_qk[:, :], 0.0).then_inc(pool_setup, 1)
            pool.memset(mask_kq[:, :], 0.0).then_inc(pool_setup, 1)
            pool.memset(half_neg[:, :], -0.5)
            pool.memset(vals[:, :, :, :], 1.0)
            pool.wait_ge(pool_setup, 3)
            pool.affine_select(out=ident[:, :], in_=ident[:, :], compare_op=ALU.not_equal, fill=1.0, base=0,
                               pattern=[[-1, P]], channel_multiplier=1).then_inc(pool_setup, 1)
            pool.affine_select(out=mask_qk[:, :], in_=mask_qk[:, :], compare_op=ALU.is_ge, fill=MASKED, base=0,
                               pattern=[[-1, P]], channel_multiplier=1)
            pool.affine_select(out=mask_kq[:, :], in_=mask_kq[:, :], compare_op=ALU.is_ge, fill=MASKED, base=0,
                               pattern=[[1, P]], channel_multiplier=-1)
            pool.iota(gnum.rearrange("p (g i) -> p g i", g=G), pattern=[[1, G], [0, FI]], base=0,
                      channel_multiplier=0, allow_small_or_imprecise_dtypes=True).then_inc(pool_setup, 1)
            pool.wait_ge(pool_setup, 5)
            pool.tensor_copy(ident_b[:, :], ident[:, :]).then_inc(consts_ready, 1)

            def program(pool, b, part, steps):
                for step in steps:
                    kind, ahead = step[0], step[1] if len(step) > 1 else 0
                    if kind in ("norm1", "norm2"):
                        i = int(kind[-1]) - 1
                        wait(pool, var_ready[i], b, ahead, 0)
                        pool.tensor_tensor(rstd, veps, half_neg[:, :], ALU.pow).then_inc(rstd_ready[i].sem, 1)
                    elif kind == "rotate":
                        g, t = step[2:]
                        wait(pool, rotated, b, ahead, 2 * g + t)
                        pool.tensor_tensor(rot[:, t, 0, :], rot[:, t, 0, :], rot[:, t, 2, :], ALU.subtract)
                        pool.tensor_tensor(rot[:, t, 3, :], rot[:, t, 3, :], rot[:, t, 1, :], ALU.add)\
                            .then_inc(rope_ready.sem, 1)
            parts(program)(pool)

        @block.scalar
        def _(sc):
            sc.wait_ge(ld_mod, 32)
            sc.activation(scT[:, :, :], ct[:, :, :], ACT.Tanh, scale=0.5).then_inc(act_setup, 1)
            sc.wait_ge(ld_k, 48)
            sc.activation(wd_hi[:, :, :], wd_st, ACT.Copy).then_inc(act_setup, 1)
            sc.activation(wk_hi[:, 0, :], wk_st[:, 0, :], ACT.Copy).then_inc(act_setup, 1)
            sc.activation(wk_hi[:, 1, :], wk_st[:, 1, :], ACT.Copy).then_inc(act_setup, 1)
            sc.activation(gw_hi[:, :, :], gw_st, ACT.Copy).then_inc(act_setup, 1)

            def program(sc, b, part, steps):
                for step in steps:
                    kind, ahead = step[0], step[1] if len(step) > 1 else 0
                    if kind == "fuse":
                        i = step[1]
                        ps = wait_full(sc, b, part, step)
                        ec, c0, n = FUSE[i]
                        sc.activation(wq_hi[:, ec, c0:c0 + n], ps[:, 0:n], ACT.Copy).then_inc(act_setup, 1)
                    elif kind == "split_ffn":
                        sc.wait_ge(ld_ffn, 16 * 5 * G)
                        for k in range(EC):
                            sc.activation(gu_hi[:, k, :], gu_st[:, k, :], ACT.Copy).then_inc(act_setup, 1)
                        sc.wait_ge(dve_setup, 13)
                    elif kind in ("turn1", "turn2"):
                        i, c = int(kind[-1]) - 1, step[2]
                        if kind == "turn1" and part == "setup" and c == 0:
                            sc.wait_ge(dve_setup, 5)
                        if i == 0:
                            wait(sc, down_added, b, ahead - 2, 1)
                        else:
                            wait(sc, mix_added, b, ahead, 1)
                        ps = wait_full(sc, b, part, step)
                        sc.activation(hf[:, c, :], ps[:, :], ACT.Identity,
                                      scale=modT[:, 4 * i + 2 + c, bass.ds(b + ahead, 1)],
                                      bias=modT[:, 4 * i + c, bass.ds(b + ahead, 1)]).then_inc(turned[i].sem, 1)
                    elif kind == "latent":
                        wait(sc, vals_ready, b, ahead - 1, 1)
                        ps = wait_full(sc, b, part, step)
                        sc.activation(ckv[:, :], ps[0:CKV, :], ACT.Copy).then_inc(latent_ready.sem, 1)
                    elif kind == "values":
                        i = step[2]
                        wait(sc, value_added, b, ahead, -1)
                        if part == "setup" and i == 0:
                            sc.wait_ge(pool_setup, 4)
                        ps = wait_full(sc, b, part, step)
                        sc.activation(vals[:, 2 * i:2 * i + 2, :, 0:HD],
                                      ps[:, :].rearrange("p (t h d) -> p t h d", t=2, h=H), ACT.Copy)\
                          .then_inc(vals_ready.sem, 1)
                    elif kind == "content":
                        g = step[2]
                        wait_parity(sc, heads_loaded, b, ahead - 1, g - 1 + NG)
                        for t in range(2):
                            ps = wait_full(sc, b, part, (*step, t))
                            sc.activation(con[:, t, :], ps[:, :], ACT.Copy).then_inc(con_ready.sem, 1)
                    elif kind == "shift":
                        g = step[2]
                        par, back, k = head_value(b, ahead - 1, g - 2 + NG)
                        wait(sc, shift_loaded[par], b, back, k)
                        ps = wait_full(sc, b, part, step)
                        sc.activation(nm[:, g % 2, :], ps[0:HG * TT, 0:P], ACT.Copy, scale=-1.0)\
                          .then_inc(nm_ready.sem, 1)
                    elif kind == "score":
                        g, n = step[2:]
                        j, h0, nh = ST_JOBS[n]
                        at, cols = PT_OFF[j] + h0 * PT_N[j], nh * PT_N[j]
                        wait(sc, value_added, b, ahead, g * TT + j - 2)
                        wait(sc, prob_filled, b, ahead, g * NST + n)
                        sc.activation(pt[:, at:at + cols], prob[(g * NST + n) % PROB_RING][:, 0:cols], ACT.Exp,
                                      scale=SCALE).then_inc(exp_ready.sem, 1)
                    elif kind == "top":
                        wait(sc, logits_shifted, b, ahead, 0)
                        sc.activation(ex[:, :, :], lg[:, :, :], ACT.Exp).then_inc(top_exp.sem, 1)
                    elif kind == "turn_w":
                        ps = wait_full(sc, b, part, step)
                        sc.activation(wT[0:NX, :], ps[0:NX, :], ACT.Copy).then_inc(wT_hi_ready.sem, 1)
                    elif kind == "gate":
                        k = step[2]
                        if k >= 2:
                            wait(sc, up_used, b, ahead, k - 2)
                        ps = wait_full(sc, b, part, step)
                        sc.activation(th[:, k % 2, :], ps[:, :], ACT.Tanh, scale=0.5).then_inc(tanh_ready.sem, 1)
            parts(program)(sc)

        @block.vector
        def _(ve):
            chained = [0]

            def chain(instruction):
                chained[0] += 1
                instruction.then_inc(setup_chain, 1)
                ve.wait_ge(setup_chain, chained[0])

            ve.memset(kh[64:P, :, :, :].bitcast(F32), 1.0)
            ve.memset(qh[64:P, :, :, :].bitcast(F32), 0.0).then_inc(key_ones, 1)
            ve.wait_ge(act_setup, 1)
            chain(ve.scalar_tensor_tensor(scT[:, :, :], scT[:, :, :], 1.0, ct[:, :, :], ALU.add, ALU.mult))
            ve.tensor_scalar(scT[:, :, :], scT[:, :, :], 0.5, None, ALU.mult).then_inc(dve_setup, 1)
            ve.wait_ge(act_setup, 5)
            ve.tensor_tensor(wd_lo[:, :, :], wd_st, wd_hi[:, :, :], ALU.subtract)
            for k in range(EC):
                ve.tensor_tensor(wk_lo[:, k, :], wk_st[:, k, :], wk_hi[:, k, :], ALU.subtract)
            ve.tensor_tensor(gw_lo[:, :, :], gw_st, gw_hi[:, :, :], ALU.subtract).then_inc(keys_split, 1)

            def program(ve, b, part, steps):
                for step in steps:
                    kind, ahead = step[0], step[1] if len(step) > 1 else 0
                    if kind == "mod":
                        ps = wait_full(ve, b, part, step)
                        v = ps[:, 0:8 * B].rearrange("p (c b) -> p c b", b=B)
                        chain(ve.tensor_copy(modT[:, :, :], v))
                        ve.sem_inc(dve_setup, 1)
                        for c in (2, 6):
                            last = ve.tensor_scalar(modT[:, c:c + 2, :], modT[:, c:c + 2, :], 1.0, None, ALU.add)
                        last.then_inc(dve_setup, 1)
                    elif kind == "gates":
                        ps = wait_full(ve, b, part, step)
                        ve.tensor_scalar(gclamp[:, 0, :], ps[0:B, :], 0.0, 2.0, ALU.is_ge, ALU.mult)
                        chain(ve.tensor_copy(gclamp[:, 1, :], ps[0:B, :]))
                        chain(ve.scalar_tensor_tensor(gclamp[:, 1, :], gclamp[:, 1, :], -1.0, gclamp[:, 1, :],
                                                      ALU.mult, ALU.max))
                        chain(ve.tensor_scalar(gclamp[:, 1, :], gclamp[:, 1, :], 0.25, None, ALU.max))
                        chain(ve.scalar_tensor_tensor(gclamp[:, 0, :], gclamp[:, 0, :], -1.0, gclamp[:, 1, :],
                                                      ALU.add, ALU.mult))
                        ve.sem_inc(dve_setup, 1)
                        ve.wait_ge(ld_small, 16 * 5)
                        ve.wait_ge(pool_setup, 5)
                        chain(ve.tensor_copy(gid, grp_i[:, :]))
                        ve.tensor_scalar(spread[:, :], gnum[0:2 * NX, :], gid, None, ALU.is_equal).then_inc(dve_setup, 1)
                    elif kind == "fuse":
                        i = step[1]
                        ps = wait_full(ve, b, part, step)
                        ec, c0, n = FUSE[i]
                        ve.wait_ge(act_setup, 6 + i)
                        ve.tensor_tensor(wq_lo[:, ec, c0:c0 + n], ps[:, 0:n], wq_hi[:, ec, c0:c0 + n],
                                         ALU.subtract).then_inc(dve_setup, 1)
                    elif kind == "split_ffn":
                        for k in range(EC):
                            ve.wait_ge(act_setup, 12 + k)
                            ve.tensor_tensor(gu_lo[:, k, :], gu_st[:, k, :], gu_hi[:, k, :], ALU.subtract)\
                              .then_inc(dve_setup, 1)
                    elif kind in ("stats1", "stats2"):
                        i = int(kind[-1]) - 1
                        if i == 0:
                            wait_alone(ve, x_loaded, b, ahead, 0)
                            for t in range(TT):
                                last = ve.bn_stats(stat[:, t, :], xn[:, t, :])
                            last.then_inc(stats_read[i].sem, 1)
                        wait_alone(ve, stats_read[i], b, ahead, 0)
                        for t in range(TT):
                            last = ve.bn_aggr(mv[:, t, :], stat[:, t, :])
                        last.then_inc(aggregated[i].sem, 1)
                        wait(ve, aggregated[i], b, ahead, 0)
                        ve.tensor_scalar(veps, mv[:, :, 1], EPS, None, ALU.add).then_inc(var_ready[i].sem, 1)
                    elif kind in ("norm1", "norm2"):
                        i = int(kind[-1]) - 1
                        src = xr if i else xn
                        wait(ve, rstd_ready[i], b, ahead, 0)
                        for t in range(TT):
                            last = ve.tensor_scalar(xn[:, t, :], src[:, t, :], mv[:, t, 0:1], rstd[:, t:t + 1],
                                                    ALU.subtract, ALU.mult)
                        last.then_inc(normed[i].sem, 1)
                    elif kind in ("turn1", "turn2"):
                        i, c = int(kind[-1]) - 1, step[2]
                        hi, lo = ((h1_hi, h1_lo), (h2_hi, h2_lo))[i]
                        wait(ve, turned[i], b, ahead, c)
                        ve.tensor_copy(hi[:, c, :], hf[:, c, :]).then_inc(hi_ready[i].sem, 1)
                        wait(ve, hi_ready[i], b, ahead, c)
                        ve.tensor_tensor(lo[:, c, :], hf[:, c, :], hi[:, c, :], ALU.subtract)\
                          .then_inc(lo_ready[i].sem, 1)
                    elif kind == "rotate":
                        g, t = step[2:]
                        if part == "setup" and t == 0:
                            ve.wait_ge(ld_tab, 32)
                        if part == "setup" and t == 1:
                            ve.wait_ge(gates_stored, 16)
                        wait_parity(ve, heads_loaded, b, ahead - 1, g - 1 + NG)
                        first = wait_full(ve, b, part, ("rope", *step[1:], 0))
                        ve.tensor_tensor(rot[:, t, 0, :], first[:, :], cos_sb[:, :], ALU.mult)
                        ve.tensor_tensor(rot[:, t, 1, :], first[:, :], sin_sb[:, :], ALU.mult)
                        second = wait_full(ve, b, part, ("rope", *step[1:], 1))
                        ve.tensor_tensor(rot[:, t, 2, :], second[:, :], sin_sb[:, :], ALU.mult)
                        ve.tensor_tensor(rot[:, t, 3, :], second[:, :], cos_sb[:, :], ALU.mult)\
                          .then_inc(rotated.sem, 1)
                    elif kind == "maxima":
                        g, i = step[2:]
                        ps = wait_full(ve, b, part, step)
                        if i == 0:
                            wait(ve, nm_ready, b, ahead, g - 2)
                        at = 0
                        pieces = MAX_JOBS[i]
                        if len(pieces) == 2 and pieces[0][1] == pieces[1][1]:
                            (h, q), w = pieces[0], (pieces[0][1] + 1) * P
                            dst = mcol[:, g % 2, :].rearrange("p (h q) -> p q h", h=HG)[:, q, h:h + 2]
                            last = ve.reduce_max(dst, ps[:, 0:2 * w].rearrange("p (h k) -> p h k", h=2), AX_X)
                        else:
                            for h, q in pieces:
                                w = (q + 1) * P
                                last = ve.reduce_max(mcol[:, g % 2, h * TT + q:h * TT + q + 1], ps[:, at:at + w], AX_X)
                                at += w
                        last.then_inc(max_read.sem, 1)
                    elif kind == "attn_out":
                        g = step[2]
                        o = ot[g % OT_BANKS]
                        wait_alone(ve, value_added, b, ahead, g * TT + TT - 1)
                        ve.stream_shuffle(norm_bc, o[:, :], [HD] * 32).then_inc(sums_moved.sem, 1)
                        wait(ve, sums_moved, b, ahead, g)
                        ve.reciprocal(norm_r, norm_bc).then_inc(sums_inverted.sem, 1)
                        wait(ve, sums_inverted, b, ahead, g)
                        ve.tensor_tensor(on[:, g, :], o[:, :], norm_r, ALU.mult).then_inc(attn_ready.sem, 1)
                    elif kind == "mix":
                        i = step[2]
                        if i == 0:
                            wait(ve, gate_loaded, b, ahead, 0)
                            wait(ve, res_loaded, b, ahead, 0)
                        ps = wait_full(ve, b, part, step)
                        gate = gate_bc[:, 0:E].unsqueeze(1).broadcast_to([P, 2, E])
                        ve.tensor_tensor(sum2[:, :, :], ps[:, :].rearrange("p (t e) -> p t e", t=2), gate, ALU.mult)\
                          .then_inc(mix_gated.sem, 1)
                        wait(ve, mix_gated, b, ahead, i)
                        ve.tensor_tensor(xr[:, 2 * i:2 * i + 2, :], xr[:, 2 * i:2 * i + 2, :], sum2[:, :, :], ALU.add)\
                          .then_inc(mix_added.sem, 1)
                        wait_alone(ve, mix_added, b, ahead, i)
                        for t in (2 * i, 2 * i + 1):
                            last = ve.bn_stats(stat[:, t, :], xr[:, t, :])
                        if i == 1:
                            last.then_inc(stats_read[1].sem, 1)
                    elif kind == "logits":
                        i = step[2]
                        ps = wait_full(ve, b, part, step)
                        ve.tensor_copy(lg[:, 2 * i:2 * i + 2, :], ps[:, 0:2 * NX].rearrange("p (t n) -> p t n", t=2))\
                          .then_inc(logits_read.sem, 1)
                    elif kind == "top":
                        bc = lambda v: v.unsqueeze(2).broadcast_to([P, TT, NX])
                        wait(ve, logits_read, b, ahead, 1)
                        ve.reduce_max(mx, lg[:, :, :], AX_X).then_inc(row_max.sem, 1)
                        wait(ve, row_max, b, ahead, 0)
                        ve.tensor_tensor(lg[:, :, :], lg[:, :, :], bc(mx), ALU.subtract).then_inc(logits_shifted.sem, 1)
                        wait_alone(ve, top_exp, b, ahead, 0)
                        for t in range(TT):
                            last = ve.max(top8[:, t, :], ex[:, t, :])
                        last.then_inc(top_found.sem, 1)
                        wait_alone(ve, top_found, b, ahead, 0)
                        for t in range(TT):
                            last = ve.match_replace(rest[:, t, :], top8[:, t, :], ex[:, t, :], -1.0)
                        last.then_inc(top_removed.sem, 1)
                        ve.reduce_sum(den, top8, AX_X).then_inc(top_summed.sem, 1)
                        wait(ve, top_summed, b, ahead, 0)
                        ve.reciprocal(rden, den).then_inc(sum_inverted.sem, 1)
                        wait(ve, top_removed, b, ahead, 0)
                        ve.scalar_tensor_tensor(rest[:, :, :], rest[:, :, :], 0.0, ex[:, :, :], ALU.is_lt, ALU.mult)\
                          .then_inc(top_kept.sem, 1)
                        wait(ve, top_kept, b, ahead, 0)
                        wait(ve, sum_inverted, b, ahead, 0)
                        ve.tensor_tensor(rest[:, :, :], rest[:, :, :], bc(rden), ALU.mult)\
                          .then_inc(weights_ready.sem, 1)
                    elif kind == "turn_w":
                        ps = wait_full(ve, b, part, step)
                        wait(ve, wT_hi_ready, b, ahead, 0)
                        ve.tensor_tensor(wT[NX:2 * NX, :], ps[0:NX, :], wT[0:NX, :], ALU.subtract)\
                          .then_inc(wT_lo_ready.sem, 1)
                    elif kind == "gate":
                        k = step[2]
                        wait(ve, tanh_ready, b, ahead, k)
                        ps = bank(part, PLACES[part][0][step])
                        ve.scalar_tensor_tensor(th[:, k % 2, :], th[:, k % 2, :], 1.0, ps[:, :], ALU.add, ALU.mult)\
                          .then_inc(gate_used.sem, 1)
                    elif kind == "up":
                        k = step[2]
                        wait(ve, gate_used, b, ahead, k)
                        ps = wait_full(ve, b, part, step)
                        ve.scalar_tensor_tensor(act[:, k, :], th[:, k % 2, :], 0.5, ps[:, :], ALU.mult, ALU.mult)\
                          .then_inc(up_used.sem, 1)
                    elif kind == "weigh":
                        k = step[2]
                        wait(ve, up_used, b, ahead, k)
                        ps = wait_full(ve, b, part, step)
                        ve.tensor_tensor(act[:, k, :], act[:, k, :], ps[:, :], ALU.mult).then_inc(inner_ready.sem, 1)
                    elif kind == "down":
                        i = step[2]
                        ps = wait_full(ve, b, part, step)
                        gate = gate_bc[:, E:2 * E].unsqueeze(1).broadcast_to([P, 2, E])
                        ve.tensor_tensor(sum2[:, :, :], ps[:, :].rearrange("p (t e) -> p t e", t=2), gate, ALU.mult)\
                          .then_inc(down_gated.sem, 1)
                        wait(ve, down_gated, b, ahead, i)
                        ve.tensor_tensor(xr[:, 2 * i:2 * i + 2, :], xr[:, 2 * i:2 * i + 2, :], sum2[:, :, :], ALU.add)\
                          .then_inc(down_added.sem, 1)
                        wait(ve, down_added, b, ahead, i)
            parts(program)(ve)

        @block.tensor
        def _(pe):
            def three(ps, whi, wlo, xhi, xlo, ready=lambda c: None):
                for c in range(EC):
                    ready(c)
                    pe.matmul(ps, wlo(c), xhi(c), start=c == 0, stop=False)
                    pe.matmul(ps, whi(c), xlo(c), start=False, stop=False)
                    last = pe.matmul(ps, whi(c), xhi(c), start=False, stop=c == EC - 1)
                return last

            def columns(hi, lo, c0, n):
                return (lambda c: hi[:, c, c0:c0 + n]), (lambda c: lo[:, c, c0:c0 + n])

            rows1 = (lambda c: h1_hi[:, c, :]), (lambda c: h1_lo[:, c, :])
            rows2 = (lambda c: h2_hi[:, c, :]), (lambda c: h2_lo[:, c, :])

            def program(pe, b, part, steps):
                for step in steps:
                    kind, ahead = step[0], step[1] if len(step) > 1 else 0
                    if kind == "mod":
                        pe.wait_ge(dve_setup, 1)
                        ps = take_bank(pe, b, part, step)
                        n = 0
                        for which in (0, 1, 3, 4):
                            for c in range(EC):
                                for k in range(EC):
                                    at = which * E + c * P
                                    last = pe.matmul(ps[:, n * B:(n + 1) * B], wmod_st[:, k, at:at + P], scT[:, k, :],
                                                     start=k == 0, stop=k == EC - 1)
                                n += 1
                        last.then_inc(full_sem, 1)
                    elif kind == "gates":
                        ps = take_bank(pe, b, part, step)
                        for i, which in enumerate((2, 5)):
                            for k in range(EC):
                                last = pe.matmul(ps[0:B, i * E:(i + 1) * E], scT[:, k, :],
                                                 wmod_st[:, k, which * E:(which + 1) * E], start=k == 0, stop=k == EC - 1)
                        last.then_inc(full_sem, 1)
                    elif kind == "fuse":
                        if step[1] == 0:
                            pe.wait_ge(ld_q, 64)
                        ps = take_bank(pe, b, part, step)
                        ec, c0, n = FUSE[step[1]]
                        pe.matmul(ps[:, 0:n], wdq_st[:, 0, ec * P:(ec + 1) * P], wu_st[:, 0, c0:c0 + n],
                                  start=True, stop=False)
                        pe.matmul(ps[:, 0:n], wdq_st[0:CQ - P, 1, ec * P:(ec + 1) * P], wu_st[0:CQ - P, 1, c0:c0 + n],
                                  start=False, stop=True).then_inc(full_sem, 1)
                    elif kind in ("turn1", "turn2"):
                        i, c = int(kind[-1]) - 1, step[2]
                        if part == "setup" and c == 0:
                            pe.wait_ge(consts_ready, 1)
                        wait(pe, normed[i], b, ahead, 0)
                        ps = take_bank(pe, b, part, step)
                        for t in range(TT):
                            last = pe.transpose(ps[:, t * P:(t + 1) * P], xn[:, t, c * P:(c + 1) * P], ident[:, :])
                        last.then_inc(full_sem, 1)
                    elif kind == "latent":
                        if part == "setup":
                            pe.wait_ge(keys_split, 1)
                            pe.wait_ge(ld_small, 16 * 5)
                        ps = take_bank(pe, b, part, step)
                        three(ps[0:CKV, :], *columns(wd_hi, wd_lo, 0, CKV), *rows1,
                              ready=lambda c: wait(pe, lo_ready[0], b, ahead, c)).then_inc(full_sem, 1)
                    elif kind == "rope":
                        g, t = step[2:]
                        hi, lo = ((wk_hi, wk_lo), (wq_hi, wq_lo))[t]
                        if part == "setup" and t == 1:
                            pe.wait_ge(dve_setup, 11)
                        for half in range(2):
                            ps = take_bank(pe, b, part, (*step, half))
                            three(ps[:, :], *columns(hi, lo, g * NROPE + half * P, P), *rows1).then_inc(full_sem, 1)
                    elif kind == "content":
                        g = step[2]
                        wait(pe, latent_ready, b, ahead, 0)
                        ps = take_bank(pe, b, part, (*step, 0))
                        pe.matmul(ps[:, :], wuk[:, g * HG * HD:(g + 2) * HG * HD], ckv[:, :], start=True, stop=True)\
                          .then_inc(full_sem, 1)
                        ps = take_bank(pe, b, part, (*step, 1))
                        three(ps[:, :], *columns(wq_hi, wq_lo, NG * NROPE + g * HG * HD, P), *rows1)\
                            .then_inc(full_sem, 1)
                    elif kind == "values":
                        i = step[2]
                        ps = take_bank(pe, b, part, step)
                        for t in range(2):
                            tok = (2 * i + t) * P
                            last = pe.matmul(ps[:, t * E:(t + 1) * E], ckv[:, tok:tok + P], wuv[:, :],
                                             start=True, stop=True)
                        last.then_inc(full_sem, 1)
                    elif kind == "maxima":
                        g, i = step[2:]
                        if i == 0:
                            wait_parity(pe, heads_loaded, b, ahead, g)
                        ps = take_bank(pe, b, part, step)
                        at, par = 0, g % 2
                        for h, q in MAX_JOBS[i]:
                            w = (q + 1) * P
                            pe.matmul(ps[:, at:at + w], qh[0:DK, par, h, q * P:(q + 1) * P], kh[0:DK, par, h, 0:w],
                                      start=True, stop=False)
                            last = pe.matmul(ps[:, at + q * P:at + w], ident_b[:, :], mask_qk[:, :],
                                             start=False, stop=True)
                            at += w
                        last.then_inc(full_sem, 1)
                    elif kind == "shift":
                        g = step[2]
                        wait(pe, max_read, b, ahead, g * NMAX + NMAX - 1)
                        ps = take_bank(pe, b, part, step)
                        pe.transpose(ps[0:HG * TT, 0:P], mcol[:, g % 2, :], ident[:, :]).then_inc(full_sem, 1)
                    elif kind == "score":
                        g, n = step[2:]
                        j, h0, nh = ST_JOBS[n]
                        par = g % 2
                        if n == 0:
                            p_, a_, k_ = head_value(b, ahead, g)
                            wait(pe, shift_loaded[p_], b, a_, k_)
                        ps = prob[(g * NST + n) % PROB_RING]
                        wait(pe, exp_ready, b, ahead, g * NST + n - PROB_RING)
                        for i in range(nh):
                            h, at = h0 + i, i * PT_N[j]
                            pe.matmul(ps[:, at:at + PT_N[j]], kh[:, par, h, j * P:(j + 1) * P].bitcast(F32),
                                      qh[:, par, h, j * P:S].bitcast(F32), start=True, stop=False)
                            last = pe.matmul(ps[:, at:at + P], ident_b[:, :], mask_kq[:, :], start=False, stop=True)
                        last.then_inc(prob_sem, 1)
                    elif kind == "value":
                        g, j = step[2:]
                        if j == 0:
                            wait(pe, vals_ready, b, ahead, 1)
                            wait(pe, attn_ready, b, ahead, g - OT_BANKS)
                        jobs = [n for n in range(NST) if ST_JOBS[n][0] == j]
                        wait(pe, exp_ready, b, ahead, g * NST + jobs[-1])
                        o = ot[g % OT_BANKS]
                        for h in range(HG):
                            at = PT_OFF[j] + h * PT_N[j]
                            last = pe.matmul(o[32 * h:32 * h + 32, j * P:S], vals[:, j, HG * g + h, :],
                                             pt[:, at:at + PT_N[j]], start=j == 0, stop=j == TT - 1)
                        last.then_inc(value_added.sem, 1)
                    elif kind == "mix":
                        i = step[2]
                        ps = take_bank(pe, b, part, step)
                        for t in range(2):
                            tok = (2 * i + t) * P
                            for g in range(NG):
                                if i == 0 and t == 0:
                                    wait(pe, attn_ready, b, ahead, g)
                                last = pe.matmul(ps[:, t * E:(t + 1) * E], on[:, g, tok:tok + P], wo[:, g, :],
                                                 start=g == 0, stop=g == NG - 1)
                        last.then_inc(full_sem, 1)
                    elif kind == "logits":
                        i = step[2]
                        ps = take_bank(pe, b, part, step)
                        for t in range(2):
                            tok = (2 * i + t) * P
                            last = three(ps[:, t * NX:(t + 1) * NX],
                                         lambda c: h2_hi[:, c, tok:tok + P], lambda c: h2_lo[:, c, tok:tok + P],
                                         lambda c: gw_hi[:, c, :], lambda c: gw_lo[:, c, :],
                                         ready=lambda c: wait(pe, lo_ready[1], b, ahead, c))
                        last.then_inc(full_sem, 1)
                    elif kind in ("gate", "up"):
                        k = step[2]
                        if isinstance(b, int) and b == 0 and kind == "gate" and k == 0:
                            pe.wait_ge(dve_setup, 13)
                        ps = take_bank(pe, b, part, step)
                        at = (kind == "up") * G * FI + k * P
                        three(ps[:, :], *columns(gu_hi, gu_lo, at, P), *rows2).then_inc(full_sem, 1)
                    elif kind == "turn_w":
                        wait(pe, weights_ready, b, ahead, 0)
                        ps = take_bank(pe, b, part, step)
                        for t in range(TT):
                            last = pe.transpose(ps[0:NX, t * P:(t + 1) * P], rest[:, t, :], ident[:, :])
                        last.then_inc(full_sem, 1)
                    elif kind == "weigh":
                        k = step[2]
                        wait(pe, wT_lo_ready, b, ahead, 0)
                        ps = take_bank(pe, b, part, step)
                        pe.matmul(ps[:, :], spread[:, k * P:(k + 1) * P], wT[:, :], start=True, stop=True)\
                          .then_inc(full_sem, 1)
                    elif kind == "down":
                        i = step[2]
                        ps = take_bank(pe, b, part, step)
                        for t in range(2):
                            tok = (2 * i + t) * P
                            for k in range(FT):
                                if i == 0 and t == 0:
                                    wait(pe, inner_ready, b, ahead, k)
                                last = pe.matmul(ps[:, t * E:(t + 1) * E], act[:, k, tok:tok + P], dn[:, k, :],
                                                 start=k == 0, stop=k == FT - 1)
                        last.then_inc(full_sem, 1)
            parts(program)(pe)


_OUT = (B, S, E)


def kernel(L0_attn_x, L0_attn_w_dq, L0_attn_w_uq, L0_attn_w_dkv, L0_attn_w_uk, L0_attn_w_uv, L0_attn_w_qr,
           L0_attn_w_kr, L0_attn_w_out, L0_ffn_gate_weight, L0_ffn_gate_up_proj, L0_ffn_down_proj,
           L0_ffn_merge_groups, L0_ffn_dominant_experts, L0_c, L0_wmod):
    import concourse.bacc as bacc
    from concourse.bass_utils import run_bass_kernel_spmd

    def rope_rows(w):
        w = np.asarray(w)
        return w.reshape(NG, HG, 2, HALF, w.shape[1]).transpose(0, 2, 3, 1, 4).reshape(NG * NROPE, w.shape[1])

    def content_rows(w):
        w = np.asarray(w)
        return w.reshape(NG, HG, HD, w.shape[1]).transpose(0, 2, 1, 3).reshape(H * HD, w.shape[1])

    inv_freq = (1.0 / 10000.0 ** (np.arange(0, RD, 2, dtype=np.float32) / np.float32(RD))).astype(np.float32)
    angle = inv_freq[:, None] * np.arange(S, dtype=np.float32)[None, :]
    wo = np.asarray(L0_attn_w_out).T.reshape(NG, HG, HD, E)
    data = {
        "x": np.asarray(L0_attn_x),
        "wu_t": np.concatenate([rope_rows(L0_attn_w_qr), content_rows(L0_attn_w_uq)]).T,
        "w_dq": np.asarray(L0_attn_w_dq),
        "wk_t": rope_rows(L0_attn_w_kr).T,
        "wdkv_t": np.asarray(L0_attn_w_dkv).T,
        "wuk_t": content_rows(L0_attn_w_uk).T,
        "wuv_t": np.asarray(L0_attn_w_uv).T,
        "wo_p": np.concatenate([wo, np.zeros_like(wo)], axis=2).reshape(NG, P, E),
        "gw_t": np.asarray(L0_ffn_gate_weight).T,
        "gup_t": np.asarray(L0_ffn_gate_up_proj).transpose(0, 2, 1),
        "dn_t": np.asarray(L0_ffn_down_proj).transpose(0, 2, 1),
        "groups": np.asarray(L0_ffn_merge_groups).reshape(NX, 1),
        "chosen": np.asarray(L0_ffn_dominant_experts).reshape(1, G),
        "c_t": np.asarray(L0_c).T,
        "wmod": np.asarray(L0_wmod),
        "cos_t": np.repeat(np.cos(angle), HG, axis=0),
        "sin_t": np.repeat(np.sin(angle), HG, axis=0),
    }
    nc = bacc.Bacc("TRN2", target_bir_lowering=False, num_devices=1)
    arrays, args = {}, []
    for name, a in data.items():
        a = np.ascontiguousarray(a)
        arrays[f"{name}_dram"] = a
        args.append(nc.dram_tensor(f"{name}_dram", a.shape, mybir.dt.from_np(a.dtype), kind="ExternalInput").ap())
    out = nc.dram_tensor("out_dram", _OUT, F32, kind="ExternalOutput").ap()
    block_program(nc, *args, out)
    r = run_bass_kernel_spmd(nc, [arrays], core_ids=[0])
    return r.results[0]["out_dram"]
```

```python
from contextlib import ExitStack

import numpy as np

import concourse.bass as bass
from concourse import mybir

ALU = mybir.AluOpType
ACT = mybir.ActivationFunctionType
AX_X = mybir.AxisListType.X
F32 = mybir.dt.float32
F32R = mybir.dt.float32r
BF16 = mybir.dt.bfloat16
I32 = mybir.dt.int32

P = 128
B, S, E = 8, 512, 256
H, HD, RD = 16, 16, 64
HALF = RD // 2
CQ, CKV = 192, 64
HG = 4
NG = H // HG
DK = RD + HD
TT = S // P
EC = E // P
SCALE = float(1.0 / np.sqrt(DK))
EPS = 1e-5
NX, TOPK, G, FI = 32, 8, 8, 96
FT = G * FI // P
NROPE = 2 * P
NQ = NG * NROPE + H * HD
MASKED = -1.0e30

ST_TILES = []
for _q0 in range(0, S, 2 * P):
    for _j in range(_q0 // P + 2):
        _from = max(_q0, _j * P)
        ST_TILES.append((_j, _from, _q0 + 2 * P - _from, _j * P >= _q0))
NTILE = len(ST_TILES)
PT_COLS = HG * 2 * P
PT_RING = 2
ST_JOBS = [(u, h, min(HG, 512 // t[2])) for u, t in enumerate(ST_TILES) for h in range(0, HG, min(HG, 512 // t[2]))]
NST = len(ST_JOBS)
MAX_JOBS = []
for _h in (0, 2):
    MAX_JOBS += [[(_h, 3)], [(_h, 0), (_h, 2)], [(_h + 1, 3)], [(_h + 1, 0), (_h + 1, 2)], [(_h, 1), (_h + 1, 1)]]
NMAX = len(MAX_JOBS)
MAX_FROM = 4
FULL_RING, PROB_RING, OT_BANKS = 4, 2, 2
INNER_RING = 4
HV = HD + 1
FUSE = [(c, at, min(512, NQ - at)) for c in range(EC) for at in range(0, NQ, 512)]


def project_steps(ahead, g, between=()):
    out = [("rope", ahead, g, 0), ("rotate", ahead, g, 0), *between, ("rope", ahead, g, 1), ("rotate", ahead, g, 1)]
    return out + ([("content", ahead, g)] if g % 2 == 0 else [])


def attend_steps(g, maxima):
    out, at = [], 0
    for n in range(NST):
        out.append(("score", 0, g, n))
        u = ST_JOBS[n][0]
        if u > 0 and (n + 1 == NST or ST_JOBS[n + 1][0] > u):
            out.append(("value", 0, g, u - 1))
        if n >= MAX_FROM:
            take = (len(maxima) * (n - MAX_FROM + 1)) // (NST - MAX_FROM)
            out += maxima[at:take]
            at = take
    return out + [("value", 0, g, NTILE - 1)]


def all_maxima(ahead, g):
    return [("maxima", ahead, g, i) for i in range(NMAX)]


def setup_steps():
    out = [("stats1", 0)] + [("fuse", i) for i in range(len(FUSE))]
    out += [("silu",), ("mod",), ("gates",), ("norm1", 0), ("split_keys",), ("turn1", 0, 0), ("turn1", 0, 1)]
    out += [("latent", 0)] + project_steps(0, 0) + [("heads", 0, 0), ("values", 0, 0), ("values", 0, 1)]
    out += project_steps(0, 1) + [("heads", 0, 1)] + all_maxima(0, 0)
    return out + [("spread",)] + project_steps(0, 2, [("shift", 0, 0)]) + [("split_ffn",)]


def body_steps(last):
    def next_batch(*steps):
        return [] if last else list(steps)

    out = [("loads", 0)] + next_batch(("load_next", 1)) + attend_steps(0, all_maxima(0, 1))
    out += [("shift", 0, 1), ("heads", 0, 2)] + project_steps(0, 3) + [("attn_out", 0, 0)]
    out += next_batch(("stats1", 1)) + attend_steps(1, all_maxima(0, 2)) + [("shift", 0, 2), ("heads", 0, 3)]
    out += next_batch(("norm1", 1), ("turn1", 1, 0), ("turn1", 1, 1)) + [("attn_out", 0, 1)]
    out += next_batch(("latent", 1), *project_steps(1, 0))
    out += attend_steps(2, all_maxima(0, 3)) + [("shift", 0, 3)] + next_batch(("heads", 1, 0))
    out += next_batch(*project_steps(1, 1)) + [("attn_out", 0, 2)]
    out += attend_steps(3, next_batch(*all_maxima(1, 0))) + next_batch(("shift", 1, 0), ("heads", 1, 1))
    out += [("attn_out", 0, 3)]
    out += next_batch(("values", 1, 0), ("values", 1, 1), ("rope", 1, 2, 0), ("rotate", 1, 2, 0))
    out += [("mix", 0, 0), ("mix", 0, 1), ("stats2", 0), ("norm2", 0)]
    out += next_batch(("content", 1, 2)) + [("turn2", 0, 0), ("turn2", 0, 1)]
    out += next_batch(("rope", 1, 2, 1), ("rotate", 1, 2, 1))
    out += [("logits", 0, 0), ("logits", 0, 1), ("top", 0)]
    out += [("gate", 0, 0), ("up", 0, 0), ("gate", 0, 1), ("up", 0, 1), ("turn_w", 0), ("gate", 0, 2), ("up", 0, 2)]
    for k in range(3, FT):
        out += [("weigh", 0, k - 3), ("gate", 0, k), ("up", 0, k), ("down", 0, k - 3)]
    for k in range(FT - 3, FT):
        out.append(("weigh", 0, k))
    return out + [("down", 0, k) for k in range(FT - 3, FT)] + [("join", 0, 0), ("join", 0, 1), ("store", 0)]


def banks_of(step):
    kind = step[0]
    if kind in ("rope", "content"):
        return 2
    return int(kind in ("mod", "gates", "turn1", "turn2", "fuse", "latent", "values", "maxima", "shift",
                        "logits", "gate", "up", "turn_w", "weigh"))


def ring_places(steps):
    place, n = {}, 0
    for s in steps:
        for i in range(banks_of(s)):
            place[(*s, i) if banks_of(s) > 1 else s] = n
            n += 1
    return place, n


SETUP, FIRST, LAST = setup_steps(), body_steps(False), body_steps(True)
PLACES = {}
for _name, _steps in (("setup", SETUP), ("body", FIRST), ("last", LAST)):
    PLACES[_name] = ring_places(_steps)
NSETUP, NBODY = PLACES["setup"][1], PLACES["body"][1]
assert NBODY % FULL_RING == 0


class Count:

    def __init__(self, sem, per, by=1):
        self.sem, self.per, self.by = sem, per, by

    def at(self, b, ahead, k):
        return b * (self.per * self.by) + (ahead * self.per + k + 1) * self.by


def block_program(nc, x, wu_t, w_dq, wk_t, wdkv_t, wuk_t, wuv_t, wo_p, gw_t, gup_t, dn_t, groups, chosen,
                  c_t, wmod, cos_t, sin_t, out):
    gates_dram = nc.dram_tensor("gates_scratch", [B, 2 * E], F32, kind="Internal").ap()
    ctx = ExitStack()
    with ctx:
        def sb(name, shape, dt=F32):
            return ctx.enter_context(nc.sbuf_tensor(name, shape, dt))

        def sem(name):
            return ctx.enter_context(nc.semaphore(name))

        wq_hi, wq_lo = sb("wq_hi", [P, EC, NQ], F32R), sb("wq_lo", [P, EC, NQ], F32R)
        wk_hi, wk_lo = sb("wk_hi", [P, EC, NG * NROPE], F32R), sb("wk_lo", [P, EC, NG * NROPE], F32R)
        wd_hi, wd_lo = sb("wd_hi", [P, EC, CKV], F32R), sb("wd_lo", [P, EC, CKV], F32R)
        gu_hi, gu_lo = sb("gu_hi", [P, EC, 2 * G * FI], F32R), sb("gu_lo", [P, EC, 2 * G * FI], F32R)
        gw_hi, gw_lo = sb("gw_hi", [P, EC, NX], F32R), sb("gw_lo", [P, EC, NX], F32R)
        wuk, wuv = sb("wuk", [CKV, E]), sb("wuv", [CKV, E])
        wo = sb("wo", [P, NG, E])
        dn = sb("dn", [P, FT, E])
        spread = sb("spread", [2 * NX, G * FI], F32R)
        table = sb("table", [P, 2, S])
        modT = sb("modT", [P, 8, B])
        gate_bc = sb("gate_bc", [P, 2 * E])
        ident, ident_b = sb("ident", [P, P]), sb("ident_b", [P, P], BF16)
        mask_qk, mask_kq = sb("mask_qk", [P, P], BF16), sb("mask_kq", [P, P], BF16)
        half_neg = sb("half_neg", [P, TT])
        xn = sb("xn", [P, TT, E])
        xr = sb("xr", [P, TT, E])
        hf = xn[:, :, :].rearrange("p (c t) e -> p c (t e)", c=EC)
        h1_hi, h1_lo = sb("h1_hi", [P, EC, S], F32R), sb("h1_lo", [P, EC, S], F32R)
        ckv = sb("ckv", [CKV, S])
        vals = sb("vals", [P, TT, H * HV + 32 - HV])
        h2_hi, h2_lo = sb("h2_hi", [P, EC, S], F32R), sb("h2_lo", [P, EC, S], F32R)
        rot = sb("rot", [P, 2, 2, 4, S])
        con = sb("con", [P, 2, 2, S])
        qh = sb("qh", [P, 2, HG, S], F32R)
        kh = sb("kh", [P, 2, HG, S], F32R)
        pt = sb("pt", [P, PT_RING * PT_COLS])
        inner = pt[:, :].rearrange("p (k s) -> p k s", k=INNER_RING)
        on = sb("on", [P, NG, S])
        small = sb("small", [P, 128])
        sum2 = hf[:, 0, :].rearrange("p (t e) -> p t e", t=2)
        wT = sb("wT", [2 * NX, S], F32R)
        mcol = sb("mcol", [P, 2, HG * TT])
        nm = sb("nm", [HG * TT, 2, P])
        stat, mv = small[:, 0:24].rearrange("p (t k) -> p t k", t=TT), small[:, 24:32].rearrange("p (t k) -> p t k", t=TT)
        veps, rstd = small[:, 32:36], small[:, 36:40]
        lg = sb("lg", [P, TT, NX])
        ex = sb("ex", [P, TT, NX])
        rest = sb("rest", [P, TT, NX])
        top8 = small[:, 40:72].rearrange("p (t k) -> p t k", t=TT)
        mx, den, rden = small[:, 72:76], small[:, 76:80], small[:, 80:84]
        scT = sb("scT", [P, EC, B])
        ct = sb("ct", [P, EC, B])
        gid = small[0:2 * NX, 100:101]
        idx_sb = sb("idx_sb", [1, G], I32)
        grp_i = sb("grp_i", [2 * NX, 1], I32)
        gclamp = rot[0:B, 1, 1, 2:4, :]
        def flat(tile, dims="p a b s"):
            return tile.rearrange(f"{dims} -> {dims[0]} ({dims[2:]})")

        gu_st = [room[:, 0:2 * G * FI] for room in (pt[:, :], flat(on[:, :, :], "p g s"))]
        wk_st = [flat(xr[:, :, :], "p t e"), flat(con[:, :, :, :])[:, 0:NG * NROPE]]
        gnum = flat(con[:, :, :, :])[:, NG * NROPE:NG * NROPE + G * FI]
        rot_flat, at = flat(rot[:, :, :, :, :], "p a b k s"), [0]

        def staged(chunks, n):
            at[0] += chunks * n
            return rot_flat[:, at[0] - chunks * n:at[0]].rearrange("p (c n) -> p c n", c=chunks)

        wu_st, wdq_st, wd_st, gw_st = staged(2, NQ), staged(2, E), staged(EC, CKV), staged(EC, NX)
        wmod_st = staged(EC, 6 * E)
        assert at[0] <= (2 * 2 * 4 - 2) * S

        full = [ctx.enter_context(nc.psum_tensor(f"full{i}", [P, 512], F32)) for i in range(FULL_RING)]
        prob = [ctx.enter_context(nc.psum_tensor(f"prob{i}", [P, 512], F32)) for i in range(PROB_RING)]
        ot = [ctx.enter_context(nc.psum_tensor(f"ot{i}", [P, 512], F32)) for i in range(OT_BANKS)]

        ld_x, ld_mod, ld_q, ld_k, ld_tab, ld_small, ld_ffn, ld_idx = (
            sem(n) for n in ("ld_x", "ld_mod", "ld_q", "ld_k", "ld_tab", "ld_small", "ld_ffn", "ld_idx"))
        x_loaded = Count(sem("x_loaded"), 1, 16)
        res_loaded = Count(sem("res_loaded"), 1, 16)
        gate_loaded = Count(sem("gate_loaded"), 1, 16)
        gates_stored = sem("gates_stored")
        stored = Count(sem("stored"), 1, 16)
        NHD = 6
        heads_loaded = [Count(sem(f"heads_loaded{i}"), NG // 2, 16 * NHD) for i in range(2)]
        shift_loaded = [Count(sem(f"shift_loaded{i}"), NG // 2, 16) for i in range(2)]
        full_sem, prob_sem = sem("full_filled"), sem("prob_filled")
        prob_filled = Count(prob_sem, NG * NST)
        value_added = Count(sem("value_added"), NG * NTILE)
        mix_filled = Count(sem("mix_filled"), 2)
        down_done = Count(sem("down_done"), FT)
        stats_read = [Count(sem(f"stats{i}_read"), 1) for i in (1, 2)]
        aggregated = [Count(sem(f"aggregated{i}"), 1) for i in (1, 2)]
        var_ready = [Count(sem(f"var{i}_ready"), 1) for i in (1, 2)]
        normed = [Count(sem(f"normed{i}"), 1) for i in (1, 2)]
        hi_ready = [Count(sem(f"h{i}_hi_ready"), EC) for i in (1, 2)]
        lo_ready = [Count(sem(f"h{i}_lo_ready"), EC) for i in (1, 2)]
        rotated = Count(sem("rotated"), 2 * NG)
        max_read = Count(sem("max_read"), NG * NMAX)
        sums_moved = Count(sem("sums_moved"), NG)
        sums_inverted = Count(sem("sums_inverted"), NG)
        attn_ready = Count(sem("attn_ready"), NG)
        mix_gated = Count(sem("mix_gated"), 2)
        mix_added = Count(sem("mix_added"), 2)
        logits_read = Count(sem("logits_read"), 2)
        row_max = Count(sem("row_max"), 1)
        logits_shifted = Count(sem("logits_shifted"), 1)
        top_found = Count(sem("top_found"), 1)
        top_removed = Count(sem("top_removed"), 1)
        top_summed = Count(sem("top_summed"), 1)
        sum_inverted = Count(sem("sum_inverted"), 1)
        top_kept = Count(sem("top_kept"), 1)
        weights_ready = Count(sem("weights_ready"), 1)
        wT_lo_ready = Count(sem("wT_lo_ready"), 1)
        gate_used = Count(sem("gate_used"), FT)
        up_used = Count(sem("up_used"), FT)
        inner_ready = Count(sem("inner_ready"), FT)
        down_gated = Count(sem("down_gated"), 2)
        down_added = Count(sem("down_added"), 2)
        keys_split, key_ones = sem("keys_split"), sem("key_ones")
        silu_ready, mod_read, mod_ready, gates_read = (sem(n) for n in ("silu_ready", "mod_read", "mod_ready", "gates_read"))
        gates_ready, spread_ready, fuse_read, ffn_split = (
            sem(n) for n in ("gates_ready", "spread_ready", "fuse_read", "ffn_split"))
        waits_passed = sem("waits_passed")
        setup_chain = sem("setup_chain")
        rstd_ready = [Count(sem(f"rstd{i}_ready"), 1) for i in (1, 2)]
        rope_ready = Count(sem("rope_ready"), 2 * NG)
        consts_ready, pool_setup = sem("consts_ready"), sem("pool_setup")
        turned = [Count(sem(f"h{i}_modulated"), EC) for i in (1, 2)]
        latent_ready = Count(sem("latent_ready"), 1)
        vals_ready = Count(sem("vals_ready"), 2)
        con_ready = Count(sem("con_ready"), NG)
        nm_ready = Count(sem("nm_ready"), NG)
        exp_ready = Count(sem("exp_ready"), NG * NST)
        top_exp = Count(sem("top_exp"), 1)
        wT_hi_ready = Count(sem("wT_hi_ready"), 1)
        tanh_ready = Count(sem("tanh_ready"), FT)
        tanh_c_ready, keys_hi_ready, fuse_hi_ready, ffn_hi_ready = (
            sem(n) for n in ("tanh_c_ready", "keys_hi_ready", "fuse_hi_ready", "ffn_hi_ready"))

        def full_value(b, part, place):
            if part == "setup":
                return place + 1
            return b * NBODY + (NSETUP + place + 1)

        def bank(part, place):
            return full[(place if part == "setup" else NSETUP + place) % FULL_RING]

        def wait_full(e, b, part, step):
            place = PLACES[part][0][step]
            e.wait_ge(full_sem, full_value(b, part, place))
            return bank(part, place)

        def wait(e, count, b, ahead, k):
            v = count.at(b, ahead, k)
            if not isinstance(v, int) or v > 0:
                e.wait_ge(count.sem, v)

        def wait_alone(e, count, b, ahead, k):
            wait(e, count, b, ahead, k)
            e.sem_inc(waits_passed, 1)

        def reader(step):
            kind, ahead = step[0], step[1] if len(step) > 1 else 0
            return {
                "turn1": lambda: (turned[0], ahead, step[2]),
                "turn2": lambda: (turned[1], ahead, step[2]),
                "latent": lambda: (latent_ready, ahead, 0),
                "values": lambda: (vals_ready, ahead, step[2]),
                "rope": lambda: (rotated, ahead, 2 * step[2] + step[3]),
                "content": lambda: (con_ready, ahead, step[2] + step[3]),
                "maxima": lambda: (max_read, ahead, NMAX * step[2] + step[3]),
                "shift": lambda: (nm_ready, ahead, step[2]),
                "logits": lambda: (logits_read, ahead, step[2]),
                "gate": lambda: (gate_used, ahead, step[2]),
                "up": lambda: (up_used, ahead, step[2]),
                "turn_w": lambda: (wT_lo_ready, ahead, 0),
                "weigh": lambda: (inner_ready, ahead, step[2]),
            }[kind]()

        ORDER = {part: sorted(PLACES[part][0], key=PLACES[part][0].get) for part in PLACES}
        SETUP_READ = {("mod",): (mod_read, 1), ("gates",): (gates_read, 1),
                      **{("fuse", i): (fuse_read, i + 1) for i in range(len(FUSE))}}

        def take_bank(e, b, part, step):
            place = PLACES[part][0][step]
            back = place - FULL_RING
            if back >= 0:
                prev, shift = ORDER[part][back], 0
            elif part == "setup":
                prev = None
            elif isinstance(b, int) and b == 0:
                prev, shift = ORDER["setup"][back], 0
            else:
                prev, shift = ORDER["body"][back], -1
            if prev is not None:
                if prev in SETUP_READ:
                    e.wait_ge(*SETUP_READ[prev])
                else:
                    count, ahead, k = reader(prev)
                    wait(e, count, b, ahead + shift, k)
            return bank(part, place)

        def parts(program):
            def run(e):
                program(e, 0, "setup", SETUP)
                program(e, 0, "body", FIRST)
                with e.Fori(1, B - 1) as b:
                    program(e, b, "body", FIRST)
                program(e, B - 1, "last", LAST)
            return run

        def head_value(b, ahead, g):
            ahead, g = ahead + g // NG, g % NG
            return g % 2, ahead, g // 2

        def wait_parity(e, counts, b, ahead, g):
            par, ahead, k = head_value(b, ahead, g)
            wait(e, counts[par], b, ahead, k)

        block = ctx.enter_context(nc.Block())

        @block.sync
        def _(sp):
            def x_rows(b, ahead):
                return x[bass.ds(b + ahead, 1), :, :].rearrange("o (t p) e -> p (o t) e", p=P)

            sp.dma_start(xn[:, :, :], x_rows(0, 0)).then_inc(x_loaded.sem, 16)
            sp.dma_start(wdq_st[:, 0, :], w_dq[0:P, :]).then_inc(ld_q, 16)
            sp.dma_start(wdq_st[0:CQ - P, 1, :], w_dq[P:CQ, :]).then_inc(ld_q, 16)
            sp.dma_start(wu_st[:, 0, :], wu_t[0:P, :]).then_inc(ld_q, 16)
            sp.dma_start(wu_st[0:CQ - P, 1, :], wu_t[P:CQ, :]).then_inc(ld_q, 16)
            sp.dma_start(ct[:, :, :], c_t.rearrange("(c p) b -> p c b", p=P)).then_inc(ld_mod, 16)
            sp.dma_start(wmod_st, wmod.rearrange("(c p) n -> p c n", p=P)).then_inc(ld_mod, 16)
            sp.dma_start(wd_st, wdkv_t.rearrange("(c p) n -> p c n", p=P)).then_inc(ld_k, 16)
            sp.dma_start(gw_st, gw_t.rearrange("(c p) n -> p c n", p=P)).then_inc(ld_k, 16)
            for c in range(EC):
                sp.dma_start(wk_st[c], wk_t[c * P:(c + 1) * P, :]).then_inc(ld_k, 16)
            sp.dma_start(table[:, 0, :], cos_t).then_inc(ld_tab, 16)
            sp.dma_start(table[:, 1, :], sin_t).then_inc(ld_tab, 16)
            sp.dma_start(idx_sb[:, :], chosen).then_inc(ld_idx, 16)
            sp.dma_start(wuk[:, :], wuk_t).then_inc(ld_small, 16)
            sp.dma_start(wuv[:, :], wuv_t).then_inc(ld_small, 16)
            sp.dma_start(wo[:, :, :], wo_p.rearrange("g p e -> p g e")).then_inc(ld_small, 16)
            sp.dma_start(grp_i[0:NX, :], groups).then_inc(ld_small, 16)
            sp.dma_start(grp_i[NX:2 * NX, :], groups).then_inc(ld_small, 16)
            sp.wait_ge(gates_ready, 1)
            sp.dma_start(gates_dram, gclamp[:, 0, :]).then_inc(gates_stored, 16)
            sp.wait_ge(gates_stored, 16)
            sp.wait_ge(key_ones, 1)

            def load_experts(experts):
                for g in experts:
                    xp = sp.value_load(idx_sb[0:1, g:g + 1], min_val=0, max_val=NX - 1)
                    src = gup_t[bass.ds(xp, 1), :, :].rearrange("o (c p) (a i) -> p (o c) a i", p=P, a=2)
                    for c in range(EC):
                        sp.dma_start(gu_st[c].rearrange("p (a g i) -> p g a i", a=2, g=G)[:, g, :, :], src[:, c, :, :])\
                          .then_inc(ld_ffn, 16)
                    for r in range(0, FI, 32):
                        row = g * FI + r
                        sp.dma_start(dn[row % P:row % P + 32, row // P, :],
                                     dn_t[bass.ds(xp, 1), r:r + 32, :].rearrange("o r e -> (o r) e")).then_inc(ld_ffn, 16)

            def program(sp, b, part, steps):
                for step in steps:
                    kind, ahead = step[0], step[1] if len(step) > 1 else 0
                    if kind == "heads":
                        g = step[2]
                        par = g % 2
                        if part == "setup":
                            if g == 0:
                                sp.wait_ge(ld_idx, 16)
                                load_experts(range(0, 2))
                            else:
                                load_experts(range(2, G))
                        wait_alone(sp, prob_filled, b, ahead, (g - 2) * NST + NST - 1)
                        for t, dst in ((0, kh), (1, qh)):
                            wait_alone(sp, rope_ready, b, ahead, 2 * g + t)
                            for half, slot in ((0, 0), (1, 2)):
                                sp.dma_start(dst[half * HALF:(half + 1) * HALF, par, :, :].bitcast(F32),
                                             rot[:, par, t, slot, :]).then_inc(heads_loaded[par].sem, 16)
                        row, pair = (g % 2) * HG * HD, g // 2
                        for t, dst in ((0, kh), (1, qh)):
                            wait_alone(sp, con_ready, b, ahead, 2 * pair + t)
                            sp.dma_start(dst[RD:DK, par, :, :].bitcast(F32), con[row:row + HG * HD, pair, t, :])\
                              .then_inc(heads_loaded[par].sem, 16)
                    elif kind == "shift":
                        g = step[2]
                        wait_alone(sp, nm_ready, b, ahead, g)
                        sp.dma_start(qh[DK:DK + 1, g % 2, :, :].bitcast(F32).rearrange("o h (q t) -> o h q t", q=TT),
                                     nm[:, g % 2, :]).then_inc(shift_loaded[g % 2].sem, 16)
                    elif kind == "loads":
                        wait_alone(sp, stored, b, ahead - 1, 0)
                        wait_alone(sp, down_gated, b, ahead - 1, 1)
                        sp.dma_start(xr[:, :, :], x_rows(b, ahead)).then_inc(res_loaded.sem, 16)
                        sp.dma_start(gate_bc[:, :], gates_dram[bass.ds(b + ahead, 1), :].broadcast_to([P, 2 * E]))\
                          .then_inc(gate_loaded.sem, 16)
                    elif kind == "load_next":
                        if isinstance(b, int) and b == 0:
                            wait_alone(sp, lo_ready[0], b, 0, 1)
                        else:
                            wait_alone(sp, lo_ready[1], b, -1, 1)
                        sp.dma_start(xn[:, :, :], x_rows(b, ahead)).then_inc(x_loaded.sem, 16)
                    elif kind == "store":
                        wait_alone(sp, down_added, b, ahead, 1)
                        sp.dma_start(out[bass.ds(b + ahead, 1), :, :].rearrange("o (t p) e -> p (o t) e", p=P),
                                     xr[:, :, :]).then_inc(stored.sem, 16)
            parts(program)(sp)
            sp.wait_ge(stored.sem, 16 * B)

        @block.gpsimd
        def _(pool):
            pool.memset(ident[:, :], 0.0).then_inc(pool_setup, 1)
            pool.memset(mask_qk[:, :], 0.0).then_inc(pool_setup, 1)
            pool.memset(mask_kq[:, :], 0.0).then_inc(pool_setup, 1)
            pool.memset(half_neg[:, :], -0.5)
            pool.memset(vals[:, :, :], 1.0)
            pool.wait_ge(pool_setup, 3)
            pool.affine_select(out=ident[:, :], in_=ident[:, :], compare_op=ALU.not_equal, fill=1.0, base=0,
                               pattern=[[-1, P]], channel_multiplier=1).then_inc(pool_setup, 1)
            pool.affine_select(out=mask_qk[:, :], in_=mask_qk[:, :], compare_op=ALU.is_ge, fill=MASKED, base=0,
                               pattern=[[-1, P]], channel_multiplier=1)
            pool.affine_select(out=mask_kq[:, :], in_=mask_kq[:, :], compare_op=ALU.is_ge, fill=MASKED, base=0,
                               pattern=[[1, P]], channel_multiplier=-1)
            pool.iota(gnum.rearrange("p (g i) -> p g i", g=G), pattern=[[1, G], [0, FI]], base=0,
                      channel_multiplier=0, allow_small_or_imprecise_dtypes=True).then_inc(pool_setup, 1)
            pool.wait_ge(pool_setup, 5)
            pool.tensor_copy(ident_b[:, :], ident[:, :]).then_inc(consts_ready, 1)

            def program(pool, b, part, steps):
                for step in steps:
                    kind, ahead = step[0], step[1] if len(step) > 1 else 0
                    if kind in ("norm1", "norm2"):
                        i = int(kind[-1]) - 1
                        wait(pool, var_ready[i], b, ahead, 0)
                        pool.tensor_tensor(rstd, veps, half_neg[:, :], ALU.pow).then_inc(rstd_ready[i].sem, 1)
                    elif kind == "rotate":
                        g, t = step[2:]
                        room = rot[:, g % 2, t, :, :]
                        wait(pool, rotated, b, ahead, 2 * g + t)
                        pool.tensor_tensor(room[:, 0, :], room[:, 0, :], room[:, 3, :], ALU.subtract)
                        pool.tensor_tensor(room[:, 2, :], room[:, 2, :], room[:, 1, :], ALU.add)\
                            .then_inc(rope_ready.sem, 1)
            parts(program)(pool)

        @block.scalar
        def _(sc):
            def program(sc, b, part, steps):
                for step in steps:
                    kind, ahead = step[0], step[1] if len(step) > 1 else 0
                    if kind == "silu":
                        sc.wait_ge(ld_mod, 32)
                        sc.activation(scT[:, :, :], ct[:, :, :], ACT.Tanh, scale=0.5).then_inc(tanh_c_ready, 1)
                    elif kind == "split_keys":
                        sc.wait_ge(ld_k, 64)
                        sc.activation(wd_hi[:, :, :], wd_st, ACT.Copy).then_inc(keys_hi_ready, 1)
                        for k in range(EC):
                            sc.activation(wk_hi[:, k, :], wk_st[k], ACT.Copy).then_inc(keys_hi_ready, 1)
                        sc.activation(gw_hi[:, :, :], gw_st, ACT.Copy).then_inc(keys_hi_ready, 1)
                    elif kind == "fuse":
                        i = step[1]
                        ps = wait_full(sc, b, part, step)
                        ec, c0, n = FUSE[i]
                        sc.activation(wq_hi[:, ec, c0:c0 + n], ps[:, 0:n], ACT.Copy).then_inc(fuse_hi_ready, 1)
                    elif kind == "split_ffn":
                        sc.wait_ge(ld_ffn, 16 * 5 * G)
                        for k in range(EC):
                            sc.activation(gu_hi[:, k, :], gu_st[k], ACT.Copy).then_inc(ffn_hi_ready, 1)
                        sc.wait_ge(ffn_split, 2)
                    elif kind in ("turn1", "turn2"):
                        i, c = int(kind[-1]) - 1, step[2]
                        if kind == "turn1" and part == "setup" and c == 0:
                            sc.wait_ge(mod_ready, 1)
                        if c == 0:
                            wait_full(sc, b, part, (kind, ahead, EC - 1))
                        ps = wait_full(sc, b, part, step)
                        sc.activation(hf[:, c, :], ps[:, :], ACT.Identity,
                                      scale=modT[:, 4 * i + 2 + c, bass.ds(b + ahead, 1)],
                                      bias=modT[:, 4 * i + c, bass.ds(b + ahead, 1)]).then_inc(turned[i].sem, 1)
                    elif kind == "latent":
                        wait(sc, vals_ready, b, ahead - 1, 1)
                        ps = wait_full(sc, b, part, step)
                        sc.activation(ckv[:, :], ps[0:CKV, :], ACT.Copy).then_inc(latent_ready.sem, 1)
                    elif kind == "values":
                        i = step[2]
                        wait(sc, value_added, b, ahead, -1)
                        if part == "setup" and i == 0:
                            sc.wait_ge(pool_setup, 4)
                        ps = wait_full(sc, b, part, step)
                        sc.activation(vals[:, 2 * i:2 * i + 2, 0:H * HV].rearrange("p t (h d) -> p t h d", h=H)[:, :, :, 0:HD],
                                      ps[:, :].rearrange("p (t h d) -> p t h d", t=2, h=H), ACT.Copy)\
                          .then_inc(vals_ready.sem, 1)
                    elif kind == "content":
                        g = step[2]
                        wait_parity(sc, heads_loaded, b, ahead - 1, g - 3 + NG)
                        for t in range(2):
                            ps = wait_full(sc, b, part, (*step, t))
                            sc.activation(con[:, g // 2, t, :], ps[:, :], ACT.Copy).then_inc(con_ready.sem, 1)
                    elif kind == "shift":
                        g = step[2]
                        par, back, k = head_value(b, ahead - 1, g - 2 + NG)
                        wait(sc, shift_loaded[par], b, back, k)
                        ps = wait_full(sc, b, part, step)
                        sc.activation(nm[:, g % 2, :], ps[0:HG * TT, 0:P], ACT.Copy, scale=-1.0)\
                          .then_inc(nm_ready.sem, 1)
                    elif kind == "score":
                        g, n = step[2:]
                        u, h0, nh = ST_JOBS[n]
                        w = ST_TILES[u][2]
                        at, cols = (u % PT_RING) * PT_COLS + h0 * w, nh * w
                        wait(sc, value_added, b, ahead, g * NTILE + u - PT_RING)
                        wait(sc, prob_filled, b, ahead, g * NST + n)
                        sc.activation(pt[:, at:at + cols], prob[(g * NST + n) % PROB_RING][:, 0:cols], ACT.Exp,
                                      scale=SCALE).then_inc(exp_ready.sem, 1)
                    elif kind == "top":
                        wait(sc, logits_shifted, b, ahead, 0)
                        sc.activation(ex[:, :, :], lg[:, :, :], ACT.Exp).then_inc(top_exp.sem, 1)
                    elif kind == "turn_w":
                        ps = wait_full(sc, b, part, step)
                        sc.activation(wT[0:NX, :], ps[0:NX, :], ACT.Copy).then_inc(wT_hi_ready.sem, 1)
                    elif kind == "gate":
                        k = step[2]
                        if k >= INNER_RING:
                            wait(sc, down_done, b, ahead, k - INNER_RING)
                        ps = wait_full(sc, b, part, step)
                        sc.activation(inner[:, k % INNER_RING, :], ps[:, :], ACT.Tanh, scale=0.5).then_inc(tanh_ready.sem, 1)
            parts(program)(sc)

        @block.vector
        def _(ve):
            chained = [0]

            def chain(instruction):
                chained[0] += 1
                instruction.then_inc(setup_chain, 1)
                ve.wait_ge(setup_chain, chained[0])

            ve.memset(kh[64:P, :, :, :].bitcast(F32), 1.0)
            ve.memset(qh[64:P, :, :, :].bitcast(F32), 0.0).then_inc(key_ones, 1)

            def program(ve, b, part, steps):
                for step in steps:
                    kind, ahead = step[0], step[1] if len(step) > 1 else 0
                    if kind == "silu":
                        ve.wait_ge(tanh_c_ready, 1)
                        chain(ve.scalar_tensor_tensor(scT[:, :, :], scT[:, :, :], 1.0, ct[:, :, :], ALU.add, ALU.mult))
                        ve.tensor_scalar(scT[:, :, :], scT[:, :, :], 0.5, None, ALU.mult).then_inc(silu_ready, 1)
                    elif kind == "split_keys":
                        ve.wait_ge(keys_hi_ready, 2 + EC)
                        ve.tensor_tensor(wd_lo[:, :, :], wd_st, wd_hi[:, :, :], ALU.subtract)
                        for k in range(EC):
                            ve.tensor_tensor(wk_lo[:, k, :], wk_st[k], wk_hi[:, k, :], ALU.subtract)
                        ve.tensor_tensor(gw_lo[:, :, :], gw_st, gw_hi[:, :, :], ALU.subtract).then_inc(keys_split, 1)
                    elif kind == "mod":
                        ps = wait_full(ve, b, part, step)
                        v = ps[:, 0:8 * B].rearrange("p (c b) -> p c b", b=B)
                        chain(ve.tensor_copy(modT[:, :, :], v))
                        ve.sem_inc(mod_read, 1)
                        for c in (2, 6):
                            last = ve.tensor_scalar(modT[:, c:c + 2, :], modT[:, c:c + 2, :], 1.0, None, ALU.add)
                        last.then_inc(mod_ready, 1)
                    elif kind == "gates":
                        ps = wait_full(ve, b, part, step)
                        ve.tensor_scalar(gclamp[:, 0, :], ps[0:B, :], 0.0, 2.0, ALU.is_ge, ALU.mult)
                        chain(ve.tensor_copy(gclamp[:, 1, :], ps[0:B, :]))
                        ve.sem_inc(gates_read, 1)
                        chain(ve.scalar_tensor_tensor(gclamp[:, 1, :], gclamp[:, 1, :], -1.0, gclamp[:, 1, :],
                                                      ALU.mult, ALU.max))
                        chain(ve.tensor_scalar(gclamp[:, 1, :], gclamp[:, 1, :], 0.25, None, ALU.max))
                        ve.scalar_tensor_tensor(gclamp[:, 0, :], gclamp[:, 0, :], -1.0, gclamp[:, 1, :],
                                                ALU.add, ALU.mult).then_inc(gates_ready, 1)
                    elif kind == "spread":
                        ve.wait_ge(ld_small, 16 * 5)
                        ve.wait_ge(pool_setup, 5)
                        chain(ve.tensor_copy(gid, grp_i[:, :]))
                        ve.tensor_scalar(spread[:, :], gnum[0:2 * NX, :], gid, None, ALU.is_equal)\
                          .then_inc(spread_ready, 1)
                    elif kind == "fuse":
                        i = step[1]
                        ps = wait_full(ve, b, part, step)
                        ec, c0, n = FUSE[i]
                        ve.wait_ge(fuse_hi_ready, i + 1)
                        ve.tensor_tensor(wq_lo[:, ec, c0:c0 + n], ps[:, 0:n], wq_hi[:, ec, c0:c0 + n],
                                         ALU.subtract).then_inc(fuse_read, 1)
                    elif kind == "split_ffn":
                        for k in range(EC):
                            ve.wait_ge(ffn_hi_ready, k + 1)
                            ve.tensor_tensor(gu_lo[:, k, :], gu_st[k], gu_hi[:, k, :], ALU.subtract)\
                              .then_inc(ffn_split, 1)
                    elif kind in ("stats1", "stats2"):
                        i = int(kind[-1]) - 1
                        if i == 0:
                            wait_alone(ve, x_loaded, b, ahead, 0)
                            for t in range(TT):
                                last = ve.bn_stats(stat[:, t, :], xn[:, t, :])
                            last.then_inc(stats_read[i].sem, 1)
                        wait_alone(ve, stats_read[i], b, ahead, 0)
                        for t in range(TT):
                            last = ve.bn_aggr(mv[:, t, :], stat[:, t, :])
                        last.then_inc(aggregated[i].sem, 1)
                        wait(ve, aggregated[i], b, ahead, 0)
                        ve.tensor_scalar(veps, mv[:, :, 1], EPS, None, ALU.add).then_inc(var_ready[i].sem, 1)
                    elif kind in ("norm1", "norm2"):
                        i = int(kind[-1]) - 1
                        src = xr if i else xn
                        wait(ve, rstd_ready[i], b, ahead, 0)
                        for t in range(TT):
                            last = ve.tensor_scalar(xn[:, t, :], src[:, t, :], mv[:, t, 0:1], rstd[:, t:t + 1],
                                                    ALU.subtract, ALU.mult)
                        last.then_inc(normed[i].sem, 1)
                    elif kind in ("turn1", "turn2"):
                        i, c = int(kind[-1]) - 1, step[2]
                        hi, lo = ((h1_hi, h1_lo), (h2_hi, h2_lo))[i]
                        wait(ve, turned[i], b, ahead, c)
                        ve.tensor_copy(hi[:, c, :], hf[:, c, :]).then_inc(hi_ready[i].sem, 1)
                        wait(ve, hi_ready[i], b, ahead, c)
                        ve.tensor_tensor(lo[:, c, :], hf[:, c, :], hi[:, c, :], ALU.subtract)\
                          .then_inc(lo_ready[i].sem, 1)
                    elif kind == "rotate":
                        g, t = step[2:]
                        if part == "setup" and (g, t) == (0, 0):
                            ve.wait_ge(ld_tab, 32)
                        if part == "setup" and (g, t) == (1, 1):
                            ve.wait_ge(gates_stored, 16)
                        wait_parity(ve, heads_loaded, b, ahead - 1, g - 2 + NG)
                        for half in range(2):
                            ps = wait_full(ve, b, part, ("rope", *step[1:], half))
                            last = ve.tensor_tensor(rot[:, g % 2, t, 2 * half:2 * half + 2, :],
                                                    ps[:, :].unsqueeze(1).broadcast_to([P, 2, S]), table[:, :, :],
                                                    ALU.mult)
                        last.then_inc(rotated.sem, 1)
                    elif kind == "maxima":
                        g, i = step[2:]
                        ps = wait_full(ve, b, part, step)
                        if i == 0:
                            wait(ve, nm_ready, b, ahead, g - 2)
                        at = 0
                        pieces = MAX_JOBS[i]
                        if len(pieces) == 2 and pieces[0][1] == pieces[1][1]:
                            (h, q), w = pieces[0], (pieces[0][1] + 1) * P
                            dst = mcol[:, g % 2, :].rearrange("p (h q) -> p q h", h=HG)[:, q, h:h + 2]
                            last = ve.reduce_max(dst, ps[:, 0:2 * w].rearrange("p (h k) -> p h k", h=2), AX_X)
                        else:
                            for h, q in pieces:
                                w = (q + 1) * P
                                last = ve.reduce_max(mcol[:, g % 2, h * TT + q:h * TT + q + 1], ps[:, at:at + w], AX_X)
                                at += w
                        last.then_inc(max_read.sem, 1)
                    elif kind == "attn_out":
                        g = step[2]
                        o = ot[g % OT_BANKS]
                        wait_alone(ve, value_added, b, ahead, g * NTILE + NTILE - 1)
                        ve.stream_shuffle(on[:, g, :], o[:, :], [HD] * 32).then_inc(sums_moved.sem, 1)
                        wait(ve, sums_moved, b, ahead, g)
                        ve.reciprocal(on[:, g, :], on[:, g, :]).then_inc(sums_inverted.sem, 1)
                        wait(ve, sums_inverted, b, ahead, g)
                        ve.tensor_tensor(on[:, g, :], o[:, :], on[:, g, :], ALU.mult).then_inc(attn_ready.sem, 1)
                    elif kind == "mix":
                        i = step[2]
                        if i == 0:
                            wait(ve, gate_loaded, b, ahead, 0)
                            wait(ve, res_loaded, b, ahead, 0)
                        wait(ve, mix_filled, b, ahead, i)
                        ps = ot[i]
                        gate = gate_bc[:, 0:E].unsqueeze(1).broadcast_to([P, 2, E])
                        ve.tensor_tensor(sum2[:, :, :], ps[:, :].rearrange("p (t e) -> p t e", t=2), gate, ALU.mult)\
                          .then_inc(mix_gated.sem, 1)
                        wait(ve, mix_gated, b, ahead, i)
                        ve.tensor_tensor(xr[:, 2 * i:2 * i + 2, :], xr[:, 2 * i:2 * i + 2, :], sum2[:, :, :], ALU.add)\
                          .then_inc(mix_added.sem, 1)
                        wait_alone(ve, mix_added, b, ahead, i)
                        for t in (2 * i, 2 * i + 1):
                            last = ve.bn_stats(stat[:, t, :], xr[:, t, :])
                        if i == 1:
                            last.then_inc(stats_read[1].sem, 1)
                    elif kind == "logits":
                        i = step[2]
                        ps = wait_full(ve, b, part, step)
                        ve.tensor_copy(lg[:, 2 * i:2 * i + 2, :], ps[:, 0:2 * NX].rearrange("p (t n) -> p t n", t=2))\
                          .then_inc(logits_read.sem, 1)
                    elif kind == "top":
                        bc = lambda v: v.unsqueeze(2).broadcast_to([P, TT, NX])
                        wait(ve, logits_read, b, ahead, 1)
                        ve.reduce_max(mx, lg[:, :, :], AX_X).then_inc(row_max.sem, 1)
                        wait(ve, row_max, b, ahead, 0)
                        ve.tensor_tensor(lg[:, :, :], lg[:, :, :], bc(mx), ALU.subtract).then_inc(logits_shifted.sem, 1)
                        wait_alone(ve, top_exp, b, ahead, 0)
                        for t in range(TT):
                            last = ve.max(top8[:, t, :], ex[:, t, :])
                        last.then_inc(top_found.sem, 1)
                        wait_alone(ve, top_found, b, ahead, 0)
                        for t in range(TT):
                            last = ve.match_replace(rest[:, t, :], top8[:, t, :], ex[:, t, :], -1.0)
                        last.then_inc(top_removed.sem, 1)
                        ve.reduce_sum(den, top8, AX_X).then_inc(top_summed.sem, 1)
                        wait(ve, top_summed, b, ahead, 0)
                        ve.reciprocal(rden, den).then_inc(sum_inverted.sem, 1)
                        wait(ve, top_removed, b, ahead, 0)
                        ve.scalar_tensor_tensor(rest[:, :, :], rest[:, :, :], 0.0, ex[:, :, :], ALU.is_lt, ALU.mult)\
                          .then_inc(top_kept.sem, 1)
                        wait(ve, top_kept, b, ahead, 0)
                        wait(ve, sum_inverted, b, ahead, 0)
                        ve.tensor_tensor(rest[:, :, :], rest[:, :, :], bc(rden), ALU.mult)\
                          .then_inc(weights_ready.sem, 1)
                    elif kind == "turn_w":
                        ps = wait_full(ve, b, part, step)
                        wait(ve, wT_hi_ready, b, ahead, 0)
                        ve.tensor_tensor(wT[NX:2 * NX, :], ps[0:NX, :], wT[0:NX, :], ALU.subtract)\
                          .then_inc(wT_lo_ready.sem, 1)
                    elif kind == "gate":
                        k = step[2]
                        wait(ve, tanh_ready, b, ahead, k)
                        ps, room = bank(part, PLACES[part][0][step]), inner[:, k % INNER_RING, :]
                        ve.scalar_tensor_tensor(room, room, 1.0, ps[:, :], ALU.add, ALU.mult)\
                          .then_inc(gate_used.sem, 1)
                    elif kind == "up":
                        k = step[2]
                        wait(ve, gate_used, b, ahead, k)
                        ps = wait_full(ve, b, part, step)
                        room = inner[:, k % INNER_RING, :]
                        ve.scalar_tensor_tensor(room, room, 0.5, ps[:, :], ALU.mult, ALU.mult)\
                          .then_inc(up_used.sem, 1)
                    elif kind == "weigh":
                        k = step[2]
                        wait(ve, up_used, b, ahead, k)
                        ps = wait_full(ve, b, part, step)
                        room = inner[:, k % INNER_RING, :]
                        ve.tensor_tensor(room, room, ps[:, :], ALU.mult).then_inc(inner_ready.sem, 1)
                    elif kind == "join":
                        i = step[2]
                        wait(ve, down_done, b, ahead, FT - 1)
                        ps = ot[i]
                        gate = gate_bc[:, E:2 * E].unsqueeze(1).broadcast_to([P, 2, E])
                        ve.tensor_tensor(sum2[:, :, :], ps[:, :].rearrange("p (t e) -> p t e", t=2), gate, ALU.mult)\
                          .then_inc(down_gated.sem, 1)
                        wait(ve, down_gated, b, ahead, i)
                        ve.tensor_tensor(xr[:, 2 * i:2 * i + 2, :], xr[:, 2 * i:2 * i + 2, :], sum2[:, :, :], ALU.add)\
                          .then_inc(down_added.sem, 1)
                        wait(ve, down_added, b, ahead, i)
            parts(program)(ve)

        @block.tensor
        def _(pe):
            def three(ps, whi, wlo, xhi, xlo, ready=lambda c: None):
                for c in range(EC):
                    ready(c)
                    pe.matmul(ps, wlo(c), xhi(c), start=c == 0, stop=False)
                    pe.matmul(ps, whi(c), xlo(c), start=False, stop=False)
                    last = pe.matmul(ps, whi(c), xhi(c), start=False, stop=c == EC - 1)
                return last

            def columns(hi, lo, c0, n):
                return (lambda c: hi[:, c, c0:c0 + n]), (lambda c: lo[:, c, c0:c0 + n])

            rows1 = (lambda c: h1_hi[:, c, :]), (lambda c: h1_lo[:, c, :])
            rows2 = (lambda c: h2_hi[:, c, :]), (lambda c: h2_lo[:, c, :])

            def program(pe, b, part, steps):
                for step in steps:
                    kind, ahead = step[0], step[1] if len(step) > 1 else 0
                    if kind == "mod":
                        pe.wait_ge(silu_ready, 1)
                        ps = take_bank(pe, b, part, step)
                        n = 0
                        for which in (0, 1, 3, 4):
                            for c in range(EC):
                                for k in range(EC):
                                    at = which * E + c * P
                                    last = pe.matmul(ps[:, n * B:(n + 1) * B], wmod_st[:, k, at:at + P], scT[:, k, :],
                                                     start=k == 0, stop=k == EC - 1)
                                n += 1
                        last.then_inc(full_sem, 1)
                    elif kind == "gates":
                        ps = take_bank(pe, b, part, step)
                        for i, which in enumerate((2, 5)):
                            for k in range(EC):
                                last = pe.matmul(ps[0:B, i * E:(i + 1) * E], scT[:, k, :],
                                                 wmod_st[:, k, which * E:(which + 1) * E], start=k == 0, stop=k == EC - 1)
                        last.then_inc(full_sem, 1)
                    elif kind == "fuse":
                        if step[1] == 0:
                            pe.wait_ge(ld_q, 64)
                        ps = take_bank(pe, b, part, step)
                        ec, c0, n = FUSE[step[1]]
                        pe.matmul(ps[:, 0:n], wdq_st[:, 0, ec * P:(ec + 1) * P], wu_st[:, 0, c0:c0 + n],
                                  start=True, stop=False)
                        pe.matmul(ps[:, 0:n], wdq_st[0:CQ - P, 1, ec * P:(ec + 1) * P], wu_st[0:CQ - P, 1, c0:c0 + n],
                                  start=False, stop=True).then_inc(full_sem, 1)
                    elif kind in ("turn1", "turn2"):
                        i, c = int(kind[-1]) - 1, step[2]
                        if part == "setup" and c == 0:
                            pe.wait_ge(consts_ready, 1)
                        wait(pe, normed[i], b, ahead, 0)
                        ps = take_bank(pe, b, part, step)
                        for t in range(TT):
                            last = pe.transpose(ps[:, t * P:(t + 1) * P], xn[:, t, c * P:(c + 1) * P], ident[:, :])
                        last.then_inc(full_sem, 1)
                    elif kind == "latent":
                        if part == "setup":
                            pe.wait_ge(keys_split, 1)
                            pe.wait_ge(ld_small, 16 * 5)
                        ps = take_bank(pe, b, part, step)
                        three(ps[0:CKV, :], *columns(wd_hi, wd_lo, 0, CKV), *rows1,
                              ready=lambda c: wait(pe, lo_ready[0], b, ahead, c)).then_inc(full_sem, 1)
                    elif kind == "rope":
                        g, t = step[2:]
                        hi, lo = ((wk_hi, wk_lo), (wq_hi, wq_lo))[t]
                        if part == "setup" and t == 1:
                            pe.wait_ge(fuse_read, len(FUSE))
                        for half in range(2):
                            ps = take_bank(pe, b, part, (*step, half))
                            three(ps[:, :], *columns(hi, lo, g * NROPE + half * P, P), *rows1).then_inc(full_sem, 1)
                    elif kind == "content":
                        g = step[2]
                        wait(pe, latent_ready, b, ahead, 0)
                        ps = take_bank(pe, b, part, (*step, 0))
                        pe.matmul(ps[:, :], wuk[:, g * HG * HD:(g + 2) * HG * HD], ckv[:, :], start=True, stop=True)\
                          .then_inc(full_sem, 1)
                        ps = take_bank(pe, b, part, (*step, 1))
                        three(ps[:, :], *columns(wq_hi, wq_lo, NG * NROPE + g * HG * HD, P), *rows1)\
                            .then_inc(full_sem, 1)
                    elif kind == "values":
                        i = step[2]
                        ps = take_bank(pe, b, part, step)
                        for t in range(2):
                            tok = (2 * i + t) * P
                            last = pe.matmul(ps[:, t * E:(t + 1) * E], ckv[:, tok:tok + P], wuv[:, :],
                                             start=True, stop=True)
                        last.then_inc(full_sem, 1)
                    elif kind == "maxima":
                        g, i = step[2:]
                        if i == 0:
                            wait_parity(pe, heads_loaded, b, ahead, g)
                        ps = take_bank(pe, b, part, step)
                        at, par = 0, g % 2
                        for h, q in MAX_JOBS[i]:
                            w = (q + 1) * P
                            pe.matmul(ps[:, at:at + w], qh[0:DK, par, h, q * P:(q + 1) * P], kh[0:DK, par, h, 0:w],
                                      start=True, stop=False)
                            last = pe.matmul(ps[:, at + q * P:at + w], ident_b[:, :], mask_qk[:, :],
                                             start=False, stop=True)
                            at += w
                        last.then_inc(full_sem, 1)
                    elif kind == "shift":
                        g = step[2]
                        wait(pe, max_read, b, ahead, g * NMAX + NMAX - 1)
                        ps = take_bank(pe, b, part, step)
                        pe.transpose(ps[0:HG * TT, 0:P], mcol[:, g % 2, :], ident[:, :]).then_inc(full_sem, 1)
                    elif kind == "score":
                        g, n = step[2:]
                        u, h0, nh = ST_JOBS[n]
                        j, q0, w, diagonal = ST_TILES[u]
                        par = g % 2
                        if n == 0:
                            wait_parity(pe, shift_loaded, b, ahead, g)
                        ps = prob[(g * NST + n) % PROB_RING]
                        wait(pe, exp_ready, b, ahead, g * NST + n - PROB_RING)
                        for i in range(nh):
                            h, at, keys = h0 + i, i * w, slice(j * P, (j + 1) * P)
                            last = pe.matmul(ps[:, at:at + w], kh[:, par, h, keys].bitcast(F32),
                                             qh[:, par, h, q0:q0 + w].bitcast(F32), start=True, stop=not diagonal)
                            if diagonal:
                                last = pe.matmul(ps[:, at:at + P], ident_b[:, :], mask_kq[:, :],
                                                 start=False, stop=True)
                        last.then_inc(prob_sem, 1)
                    elif kind == "value":
                        g, u = step[2:]
                        if u == 0:
                            wait(pe, vals_ready, b, ahead, 1)
                            wait(pe, attn_ready, b, ahead, g - OT_BANKS)
                            if g < OT_BANKS:
                                wait(pe, down_gated, b, ahead - 1, g)
                        jobs = [n for n in range(NST) if ST_JOBS[n][0] == u]
                        wait(pe, exp_ready, b, ahead, g * NST + jobs[-1])
                        o = ot[g % OT_BANKS]
                        j, q0, w, _ = ST_TILES[u]
                        final = u == NTILE - 1 or ST_TILES[u + 1][0] == 0
                        for h in range(HG):
                            at, v0 = (u % PT_RING) * PT_COLS + h * w, (HG * g + h) * HV
                            last = pe.matmul(o[32 * h:32 * h + 32, q0:q0 + w], vals[:, j, v0:v0 + 32],
                                             pt[:, at:at + w], start=j == 0, stop=final)
                        last.then_inc(value_added.sem, 1)
                    elif kind == "mix":
                        i = step[2]
                        for t in range(2):
                            tok = (2 * i + t) * P
                            for g in range(NG):
                                if (i, t) == (0, 0):
                                    wait(pe, attn_ready, b, ahead, max(g, NG - OT_BANKS))
                                last = pe.matmul(ot[i][:, t * E:(t + 1) * E], on[:, g, tok:tok + P], wo[:, g, :],
                                                 start=g == 0, stop=g == NG - 1)
                        last.then_inc(mix_filled.sem, 1)
                    elif kind == "logits":
                        i = step[2]
                        ps = take_bank(pe, b, part, step)
                        for t in range(2):
                            tok = (2 * i + t) * P
                            last = three(ps[:, t * NX:(t + 1) * NX],
                                         lambda c: h2_hi[:, c, tok:tok + P], lambda c: h2_lo[:, c, tok:tok + P],
                                         lambda c: gw_hi[:, c, :], lambda c: gw_lo[:, c, :],
                                         ready=lambda c: wait(pe, lo_ready[1], b, ahead, c))
                        last.then_inc(full_sem, 1)
                    elif kind in ("gate", "up"):
                        k = step[2]
                        if isinstance(b, int) and b == 0 and kind == "gate" and k == 0:
                            pe.wait_ge(ffn_split, EC)
                        ps = take_bank(pe, b, part, step)
                        at = (kind == "up") * G * FI + k * P
                        three(ps[:, :], *columns(gu_hi, gu_lo, at, P), *rows2).then_inc(full_sem, 1)
                    elif kind == "turn_w":
                        wait(pe, weights_ready, b, ahead, 0)
                        ps = take_bank(pe, b, part, step)
                        for t in range(TT):
                            last = pe.transpose(ps[0:NX, t * P:(t + 1) * P], rest[:, t, :], ident[:, :])
                        last.then_inc(full_sem, 1)
                    elif kind == "weigh":
                        k = step[2]
                        wait(pe, wT_lo_ready, b, ahead, 0)
                        if isinstance(b, int) and b == 0 and k == 0:
                            pe.wait_ge(spread_ready, 1)
                        ps = take_bank(pe, b, part, step)
                        pe.matmul(ps[:, :], spread[:, k * P:(k + 1) * P], wT[:, :], start=True, stop=True)\
                          .then_inc(full_sem, 1)
                    elif kind == "down":
                        k = step[2]
                        if k == 0:
                            wait(pe, mix_gated, b, ahead, 1)
                        wait(pe, inner_ready, b, ahead, k)
                        for t in range(TT):
                            last = pe.matmul(ot[t // 2][:, (t % 2) * E:(t % 2 + 1) * E],
                                             inner[:, k % INNER_RING, t * P:(t + 1) * P], dn[:, k, :],
                                             start=k == 0 and t % 2 == 0, stop=k == FT - 1 and t % 2 == 1)
                        last.then_inc(down_done.sem, 1)
            parts(program)(pe)


_OUT = (B, S, E)


def kernel(L0_attn_x, L0_attn_w_dq, L0_attn_w_uq, L0_attn_w_dkv, L0_attn_w_uk, L0_attn_w_uv, L0_attn_w_qr,
           L0_attn_w_kr, L0_attn_w_out, L0_ffn_gate_weight, L0_ffn_gate_up_proj, L0_ffn_down_proj,
           L0_ffn_merge_groups, L0_ffn_dominant_experts, L0_c, L0_wmod):
    import concourse.bacc as bacc
    from concourse.bass_utils import run_bass_kernel_spmd

    def rope_rows(w):
        w = np.asarray(w)
        return w.reshape(NG, HG, 2, HALF, w.shape[1]).transpose(0, 2, 3, 1, 4).reshape(NG * NROPE, w.shape[1])

    def content_rows(w):
        w = np.asarray(w)
        return w.reshape(NG, HG, HD, w.shape[1]).transpose(0, 2, 1, 3).reshape(H * HD, w.shape[1])

    inv_freq = (1.0 / 10000.0 ** (np.arange(0, RD, 2, dtype=np.float32) / np.float32(RD))).astype(np.float32)
    angle = inv_freq[:, None] * np.arange(S, dtype=np.float32)[None, :]
    wo = np.asarray(L0_attn_w_out).T.reshape(NG, HG, HD, E)
    data = {
        "x": np.asarray(L0_attn_x),
        "wu_t": np.concatenate([rope_rows(L0_attn_w_qr), content_rows(L0_attn_w_uq)]).T,
        "w_dq": np.asarray(L0_attn_w_dq),
        "wk_t": rope_rows(L0_attn_w_kr).T,
        "wdkv_t": np.asarray(L0_attn_w_dkv).T,
        "wuk_t": content_rows(L0_attn_w_uk).T,
        "wuv_t": np.asarray(L0_attn_w_uv).T,
        "wo_p": np.concatenate([wo, np.zeros_like(wo)], axis=2).reshape(NG, P, E),
        "gw_t": np.asarray(L0_ffn_gate_weight).T,
        "gup_t": np.asarray(L0_ffn_gate_up_proj).transpose(0, 2, 1),
        "dn_t": np.asarray(L0_ffn_down_proj).transpose(0, 2, 1),
        "groups": np.asarray(L0_ffn_merge_groups).reshape(NX, 1),
        "chosen": np.asarray(L0_ffn_dominant_experts).reshape(1, G),
        "c_t": np.asarray(L0_c).T,
        "wmod": np.asarray(L0_wmod),
        "cos_t": np.repeat(np.cos(angle), HG, axis=0),
        "sin_t": np.repeat(np.sin(angle), HG, axis=0),
    }
    nc = bacc.Bacc("TRN2", target_bir_lowering=False, num_devices=1)
    arrays, args = {}, []
    for name, a in data.items():
        a = np.ascontiguousarray(a)
        arrays[f"{name}_dram"] = a
        args.append(nc.dram_tensor(f"{name}_dram", a.shape, mybir.dt.from_np(a.dtype), kind="ExternalInput").ap())
    out = nc.dram_tensor("out_dram", _OUT, F32, kind="ExternalOutput").ap()
    block_program(nc, *args, out)
    r = run_bass_kernel_spmd(nc, [arrays], core_ids=[0])
    return r.results[0]["out_dram"]
```

```python
from contextlib import ExitStack

import numpy as np

import concourse.bass as bass
from concourse import mybir

ALU = mybir.AluOpType
ACT = mybir.ActivationFunctionType
AX_X = mybir.AxisListType.X
F32 = mybir.dt.float32
F32R = mybir.dt.float32r
BF16 = mybir.dt.bfloat16
I32 = mybir.dt.int32

P = 128
B, S, E = 8, 512, 256
H, HD, RD = 16, 16, 64
HALF = RD // 2
CQ, CKV = 192, 64
HG = 4
NG = H // HG
DK = RD + HD
TT = S // P
EC = E // P
SCALE = float(1.0 / np.sqrt(DK))
EPS = 1e-5
NX, TOPK, G, FI = 32, 8, 8, 96
FT = G * FI // P
NROPE = 2 * P
NQ = NG * NROPE + H * HD
MASKED = -1.0e30
assert TOPK == 8

ST_TILES = []
for _q0 in range(0, S, 2 * P):
    for _j in range(_q0 // P + 2):
        _from = max(_q0, _j * P)
        ST_TILES.append((_j, _from, _q0 + 2 * P - _from, _j * P >= _q0))
NTILE = len(ST_TILES)
PT_COLS = HG * 2 * P
PT_RING = 2
ST_JOBS = [(u, h, min(HG, 512 // t[2])) for u, t in enumerate(ST_TILES) for h in range(0, HG, min(HG, 512 // t[2]))]
NST = len(ST_JOBS)
MAX_JOBS = []
for _h in (0, 2):
    MAX_JOBS += [[(_h, 3)], [(_h, 2), (_h, 0)], [(_h + 1, 3)], [(_h + 1, 2), (_h + 1, 0)], [(_h, 1), (_h + 1, 1)]]
NMAX = len(MAX_JOBS)
FIRST_HALF_OUT = (9, 9, 9, 6)
MAX_FROM = 3
FULL_RING, PROB_RING, OT_BANKS = 4, 2, 2
INNER_RING = 4
HV = 2 * HD
NPAIR = NG // 2
DOWN_PIECES = [[(a, min((a // P + 1) * P, (g + 1) * FI) - a)
                for a in sorted({g * FI, (((g + 1) * FI - 1) // P) * P}) if a >= g * FI] for g in range(G)]
FUSE = [(c, at, min(512, NQ - at)) for c in range(EC) for at in range(0, NQ, 512)]


def rotate_steps(ahead, g, t):
    return [("rotate", ahead, g, t, half) for half in range(2)]


def project_steps(ahead, g, between=()):
    out = [("rope", ahead, g, 0), *between, *rotate_steps(ahead, g, 0), ("rope", ahead, g, 1), *rotate_steps(ahead, g, 1)]
    return out + ([("content", ahead, g)] if g % 2 == 0 else [])


def attend_steps(g, maxima, between={}, until=NST - 1):
    out, at = [], 0
    for n in range(NST):
        out.append(("score", 0, g, n))
        u = ST_JOBS[n][0]
        if u > 0 and (n + 1 == NST or ST_JOBS[n + 1][0] > u):
            out.append(("value", 0, g, u - 1))
        if n >= MAX_FROM:
            take = len(maxima) * (n - MAX_FROM + 1) // (until - MAX_FROM)
            out += maxima[at:take]
            at = take
        out += between.get(n, [])
        if n == FIRST_HALF_OUT[g]:
            out.append(("attn_out", 0, g, 0))
    return out


def last_value(g):
    return [("value", 0, g, NTILE - 1)]


def all_maxima(ahead, g):
    return [("maxima", ahead, g, i) for i in range(NMAX)]


def setup_steps():
    out = [("stats1", 0), ("fuse", 0), ("norm1", 0)] + [("fuse", i) for i in range(1, len(FUSE))]
    out += [("silu",), ("mod",), ("split_keys",), ("turn1", 0, 0), ("turn1", 0, 1), ("gates",)]
    out += [("latent", 0)] + project_steps(0, 0) + [("heads", 0, 0), ("values", 0, 0), ("values", 0, 1)]
    out += project_steps(0, 1) + [("heads", 0, 1)]
    out += [("rope", 0, 2, 0), *rotate_steps(0, 2, 0), ("spread",)]
    maxima = all_maxima(0, 0)
    for k in range(EC):
        out += maxima[5 * k:5 * k + 5] + [("split_ffn", k)]
    return out + [("rope", 0, 2, 1), ("shift", 0, 0), *rotate_steps(0, 2, 1), ("content", 0, 2)]


def body_steps(last):
    def next_batch(*steps):
        return [] if last else list(steps)

    out = [("loads", 0)] + next_batch(("load_next", 1))
    out += attend_steps(0, all_maxima(0, 1))
    out += [("shift", 0, 1), ("heads", 0, 2)] + next_batch(("stats1", 1)) + project_steps(0, 3, last_value(0)) + [("attn_out", 0, 0, 1)]
    between, until = ({}, NST - 3) if last else ({4: [("norm1", 1)], 7: [("turn1", 1, 0), ("turn1", 1, 1)]}, NST - 1)
    shift = [("shift", 0, 2)]
    out += attend_steps(1, all_maxima(0, 2), {**between, **({8: shift} if last else {})}, until)
    out += last_value(1) + next_batch(("latent", 1), *shift) + [("heads", 0, 3)]
    out += next_batch(*project_steps(1, 0)) + [("attn_out", 0, 1, 1)]
    shift = [("shift", 0, 3)]
    out += attend_steps(2, all_maxima(0, 3), {8: shift} if last else {}, until)
    out += next_batch(*shift, ("heads", 1, 0))
    out += next_batch(*project_steps(1, 1, last_value(2))) + ([] if not last else last_value(2)) + [("attn_out", 0, 2, 1)]
    out += attend_steps(3, next_batch(*all_maxima(1, 0))) + last_value(3) + [("attn_out", 0, 3, 1)]
    out += next_batch(("values", 1, 0), ("values", 1, 1), ("shift", 1, 0), ("heads", 1, 1))
    out += [("mix", 0, 0), ("mix", 0, 1)] + next_batch(("content", 1, 2), ("rope", 1, 2, 0))
    first, second = rotate_steps(1, 2, 0)
    out += [("stats2", 0)] + next_batch(first) + [("norm2", 0)] + next_batch(second)
    out += [("turn2", 0, 0), ("turn2", 0, 1)] + next_batch(("rope", 1, 2, 1), *rotate_steps(1, 2, 1))
    out += [("logits", 0, 0), ("logits", 0, 1), ("top", 0)]
    out += [("gate", 0, 0), ("up", 0, 0), ("gate", 0, 1), ("up", 0, 1), ("turn_w", 0), ("gate", 0, 2), ("up", 0, 2)]
    for k in range(3, FT):
        out += [("weigh", 0, k - 3), ("gate", 0, k), ("up", 0, k), ("down", 0, k - 3)]
    for k in range(FT - 3, FT):
        out.append(("weigh", 0, k))
    return out + [("down", 0, k) for k in range(FT - 3, FT)] + [("join", 0, 0), ("join", 0, 1), ("store", 0)]


def banks_of(step):
    kind = step[0]
    if kind in ("rope", "content"):
        return 2
    return int(kind in ("mod", "gates", "turn1", "turn2", "fuse", "latent", "values", "maxima", "shift",
                        "logits", "gate", "up", "turn_w", "weigh"))


def ring_places(steps):
    place, n = {}, 0
    for s in steps:
        for i in range(banks_of(s)):
            place[(*s, i) if banks_of(s) > 1 else s] = n
            n += 1
    return place, n


SETUP, FIRST, LAST = setup_steps(), body_steps(False), body_steps(True)
PLACES = {}
for _name, _steps in (("setup", SETUP), ("body", FIRST), ("last", LAST)):
    PLACES[_name] = ring_places(_steps)
NSETUP, NBODY = PLACES["setup"][1], PLACES["body"][1]
assert NBODY % FULL_RING == 0


class Count:

    def __init__(self, sem, per, by=1):
        self.sem, self.per, self.by = sem, per, by

    def at(self, b, ahead, k):
        return b * (self.per * self.by) + (ahead * self.per + k + 1) * self.by


def block_program(nc, x, wu_t, w_dq, wk_t, wdkv_t, wuk_t, wuv_t, wo_p, gw_t, gup_t, dn_t, groups, chosen,
                  c_t, wmod, cos_t, sin_t, out):
    gates_dram = nc.dram_tensor("gates_scratch", [B, 2 * E], F32, kind="Internal").ap()
    ctx = ExitStack()
    with ctx:
        def sb(name, shape, dt=F32):
            return ctx.enter_context(nc.sbuf_tensor(name, shape, dt))

        def sem(name):
            return ctx.enter_context(nc.semaphore(name))

        wq_hi, wq_lo = sb("wq_hi", [P, EC, NQ], F32R), sb("wq_lo", [P, EC, NQ], F32R)
        wk_hi, wk_lo = sb("wk_hi", [P, EC, NG * NROPE], F32R), sb("wk_lo", [P, EC, NG * NROPE], F32R)
        wd_hi, wd_lo = sb("wd_hi", [P, EC, CKV], F32R), sb("wd_lo", [P, EC, CKV], F32R)
        gu_hi, gu_lo = sb("gu_hi", [P, EC, 2 * G * FI], F32R), sb("gu_lo", [P, EC, 2 * G * FI], F32R)
        gw_hi, gw_lo = sb("gw_hi", [P, EC, NX], F32R), sb("gw_lo", [P, EC, NX], F32R)
        wuk, wuv = sb("wuk", [CKV, E]), sb("wuv", [CKV, E])
        wo = sb("wo", [P, NPAIR, E])
        dn = sb("dn", [P, FT, E])
        spread = sb("spread", [2 * NX, G * FI], F32R)
        table = sb("table", [P, 2, S])
        modT = sb("modT", [P, 8, B])
        gate_bc = sb("gate_bc", [P, 2 * E])
        ident, ident_b = sb("ident", [P, P]), sb("ident_b", [P, P], BF16)
        mask_qk, mask_kq = sb("mask_qk", [P, P], BF16), sb("mask_kq", [P, P], BF16)
        half_neg = sb("half_neg", [P, TT])
        xn = sb("xn", [P, TT, E])
        xr = sb("xr", [P, TT, E])
        hf = xn[:, :, :].rearrange("p (c t) e -> p c (t e)", c=EC)
        h1_hi, h1_lo = sb("h1_hi", [P, EC, S], F32R), sb("h1_lo", [P, EC, S], F32R)
        ckv = sb("ckv", [CKV, S])
        vals = sb("vals", [P, TT, 2, H // 2, HV])
        keep = sb("keep", [P, 2])
        h2_hi, h2_lo = sb("h2_hi", [P, EC, S], F32R), sb("h2_lo", [P, EC, S], F32R)
        rot = sb("rot", [P, 2, 2, 4, S])
        con = sb("con", [P, 2, 2, S])
        qh = sb("qh", [P, 2, HG, S], F32R)
        kh = sb("kh", [P, 2, HG, S], F32R)
        pt = sb("pt", [P, PT_RING * PT_COLS])
        inner = pt[:, :].rearrange("p (k s) -> p k s", k=INNER_RING)
        on_room = sb("on", [P, NPAIR + 1, S])
        on, norm = on_room[:, 0:NPAIR, :], on_room[:, NPAIR, :]
        small = sb("small", [P, 128])
        sum2 = hf[:, 0, :].rearrange("p (t e) -> p t e", t=2)
        wT = sb("wT", [2 * NX, S], F32R)
        mcol = sb("mcol", [P, 2, HG * TT])
        nm = sb("nm", [HG * TT, 2, P])
        stat, mv = small[:, 0:24].rearrange("p (t k) -> p t k", t=TT), small[:, 24:32].rearrange("p (t k) -> p t k", t=TT)
        veps, rstd = small[:, 32:36], small[:, 36:40]
        lg = sb("lg", [P, TT, NX])
        ex = sb("ex", [P, TT, NX])
        rest = sb("rest", [P, TT, NX])
        top8 = small[:, 40:72].rearrange("p (t k) -> p t k", t=TT)
        mx, den, rden = small[:, 72:76], small[:, 76:80], small[:, 80:84]
        scT = sb("scT", [P, EC, B])
        ct = sb("ct", [P, EC, B])
        gid = small[0:2 * NX, 100:101]
        idx_sb = sb("idx_sb", [1, G], I32)
        grp_i = sb("grp_i", [2 * NX, 1], I32)
        def flat(tile, dims="p a b s"):
            return tile.rearrange(f"{dims} -> {dims[0]} ({dims[2:]})")

        gu_st = [room[:, 0:2 * G * FI] for room in (pt[:, :], flat(on_room[:, :, :], "p g s"))]
        wk_st = [flat(xr[:, :, :], "p t e"), flat(con[:, :, :, :])[:, 0:NG * NROPE]]
        gnum = flat(con[:, :, :, :])[:, NG * NROPE:NG * NROPE + G * FI]
        rot_flat, at = flat(rot[:, :, :, :, :], "p a b k s"), [0]

        def staged(chunks, n):
            at[0] += chunks * n
            return rot_flat[:, at[0] - chunks * n:at[0]].rearrange("p (c n) -> p c n", c=chunks)

        wu_st, wdq_st, wd_st, gw_st = staged(2, NQ), staged(2, E), staged(EC, CKV), staged(EC, NX)
        wmod_st = staged(EC, 6 * E)
        gates, gates_abs = pt[0:B, 2 * G * FI:2 * G * FI + 2 * E], staged(1, 2 * E)[0:B, 0, :]
        assert at[0] <= 2 * 2 * 4 * S

        full = [ctx.enter_context(nc.psum_tensor(f"full{i}", [P, 512], F32)) for i in range(FULL_RING)]
        prob = [ctx.enter_context(nc.psum_tensor(f"prob{i}", [P, 512], F32)) for i in range(PROB_RING)]
        ot = [ctx.enter_context(nc.psum_tensor(f"ot{i}", [P, 512], F32)) for i in range(OT_BANKS)]

        ld_x, ld_mod, ld_q, ld_k, ld_tab, ld_small, ld_ffn, ld_idx = (
            sem(n) for n in ("ld_x", "ld_mod", "ld_q", "ld_k", "ld_tab", "ld_small", "ld_ffn", "ld_idx"))
        x_loaded = Count(sem("x_loaded"), 1, 16)
        res_loaded = Count(sem("res_loaded"), 1, 16)
        gate_loaded = Count(sem("gate_loaded"), 1, 16)
        gates_stored = sem("gates_stored")
        stored = Count(sem("stored"), 1, 16)
        NHD = 6
        heads_loaded = [Count(sem(f"heads_loaded{i}"), NG // 2, 16 * NHD) for i in range(2)]
        shift_loaded = [Count(sem(f"shift_loaded{i}"), NG // 2, 16) for i in range(2)]
        full_sem, prob_sem = sem("full_filled"), sem("prob_filled")
        prob_filled = Count(prob_sem, NG * NST)
        value_added = Count(sem("value_added"), NG * NTILE)
        mix_filled = Count(sem("mix_filled"), 2)
        down_done = Count(sem("down_done"), FT)
        stats_read = [Count(sem(f"stats{i}_read"), 1) for i in (1, 2)]
        aggregated = [Count(sem(f"aggregated{i}"), 1) for i in (1, 2)]
        var_ready = [Count(sem(f"var{i}_ready"), 1) for i in (1, 2)]
        normed = [Count(sem(f"normed{i}"), 1) for i in (1, 2)]
        hi_ready = [Count(sem(f"h{i}_hi_ready"), EC) for i in (1, 2)]
        lo_ready = [Count(sem(f"h{i}_lo_ready"), EC) for i in (1, 2)]
        rotated = Count(sem("rotated"), 2 * NG)
        max_read = Count(sem("max_read"), NG * NMAX)
        sums_moved = Count(sem("sums_moved"), 2 * NG)
        sums_inverted = Count(sem("sums_inverted"), 2 * NG)
        normalised = Count(sem("normalised"), 2 * NG)
        pair_ready = Count(sem("pair_ready"), 2 * NPAIR)
        mix_gated = Count(sem("mix_gated"), 2)
        mix_added = Count(sem("mix_added"), 2)
        logits_read = Count(sem("logits_read"), 2)
        row_max = Count(sem("row_max"), 1)
        logits_shifted = Count(sem("logits_shifted"), 1)
        top_found = Count(sem("top_found"), 1)
        top_removed = Count(sem("top_removed"), 1)
        top_summed = Count(sem("top_summed"), 1)
        sum_inverted = Count(sem("sum_inverted"), 1)
        top_kept = Count(sem("top_kept"), 1)
        weights_ready = Count(sem("weights_ready"), 1)
        wT_lo_ready = Count(sem("wT_lo_ready"), 1)
        gate_used = Count(sem("gate_used"), FT)
        up_used = Count(sem("up_used"), FT)
        inner_ready = Count(sem("inner_ready"), FT)
        down_gated = Count(sem("down_gated"), 2)
        down_added = Count(sem("down_added"), 2)
        keys_split, key_ones = sem("keys_split"), sem("key_ones")
        silu_ready, mod_read, mod_ready, gates_read = (sem(n) for n in ("silu_ready", "mod_read", "mod_ready", "gates_read"))
        gates_ready, spread_ready, fuse_read, ffn_split = (
            sem(n) for n in ("gates_ready", "spread_ready", "fuse_read", "ffn_split"))
        waits_passed = sem("waits_passed")
        setup_chain = sem("setup_chain")
        rstd_ready = [Count(sem(f"rstd{i}_ready"), 1) for i in (1, 2)]
        rope_ready = Count(sem("rope_ready"), 2 * NG)
        consts_ready, pool_setup = sem("consts_ready"), sem("pool_setup")
        turned = [Count(sem(f"h{i}_modulated"), EC) for i in (1, 2)]
        latent_ready = Count(sem("latent_ready"), 1)
        vals_ready = Count(sem("vals_ready"), 2)
        con_ready = Count(sem("con_ready"), NG)
        nm_ready = Count(sem("nm_ready"), NG)
        exp_ready = Count(sem("exp_ready"), NG * NST)
        top_exp = Count(sem("top_exp"), 1)
        wT_hi_ready = Count(sem("wT_hi_ready"), 1)
        tanh_ready = Count(sem("tanh_ready"), FT)
        tanh_c_ready, keys_hi_ready, fuse_hi_ready, ffn_hi_ready = (
            sem(n) for n in ("tanh_c_ready", "keys_hi_ready", "fuse_hi_ready", "ffn_hi_ready"))

        def full_value(b, part, place):
            if part == "setup":
                return place + 1
            return b * NBODY + (NSETUP + place + 1)

        def bank(part, place):
            return full[(place if part == "setup" else NSETUP + place) % FULL_RING]

        def wait_full(e, b, part, step):
            place = PLACES[part][0][step]
            e.wait_ge(full_sem, full_value(b, part, place))
            return bank(part, place)

        def wait(e, count, b, ahead, k):
            v = count.at(b, ahead, k)
            if not isinstance(v, int) or v > 0:
                e.wait_ge(count.sem, v)

        def wait_alone(e, count, b, ahead, k):
            wait(e, count, b, ahead, k)
            e.sem_inc(waits_passed, 1)

        def reader(step):
            kind, ahead = step[0], step[1] if len(step) > 1 else 0
            return {
                "turn1": lambda: (turned[0], ahead, step[2]),
                "turn2": lambda: (turned[1], ahead, step[2]),
                "latent": lambda: (latent_ready, ahead, 0),
                "values": lambda: (vals_ready, ahead, step[2]),
                "rope": lambda: (rotated, ahead, 2 * step[2] + step[3]),
                "content": lambda: (con_ready, ahead, step[2] + step[3]),
                "maxima": lambda: (max_read, ahead, NMAX * step[2] + step[3]),
                "shift": lambda: (nm_ready, ahead, step[2]),
                "logits": lambda: (logits_read, ahead, step[2]),
                "gate": lambda: (gate_used, ahead, step[2]),
                "up": lambda: (up_used, ahead, step[2]),
                "turn_w": lambda: (wT_lo_ready, ahead, 0),
                "weigh": lambda: (inner_ready, ahead, step[2]),
            }[kind]()

        ORDER = {part: sorted(PLACES[part][0], key=PLACES[part][0].get) for part in PLACES}
        SETUP_READ = {("mod",): (mod_read, 1), ("gates",): (gates_read, 1),
                      **{("fuse", i): (fuse_read, i + 1) for i in range(len(FUSE))}}

        def take_bank(e, b, part, step):
            place = PLACES[part][0][step]
            back = place - FULL_RING
            if back >= 0:
                prev, shift = ORDER[part][back], 0
            elif part == "setup":
                prev = None
            elif isinstance(b, int) and b == 0:
                prev, shift = ORDER["setup"][back], 0
            else:
                prev, shift = ORDER["body"][back], -1
            if prev is not None:
                if prev in SETUP_READ:
                    e.wait_ge(*SETUP_READ[prev])
                else:
                    count, ahead, k = reader(prev)
                    wait(e, count, b, ahead + shift, k)
            return bank(part, place)

        def parts(program):
            def run(e):
                program(e, 0, "setup", SETUP)
                program(e, 0, "body", FIRST)
                with e.Fori(1, B - 1) as b:
                    program(e, b, "body", FIRST)
                program(e, B - 1, "last", LAST)
            return run

        def head_value(b, ahead, g):
            ahead, g = ahead + g // NG, g % NG
            return g % 2, ahead, g // 2

        def wait_parity(e, counts, b, ahead, g):
            par, ahead, k = head_value(b, ahead, g)
            wait(e, counts[par], b, ahead, k)

        block = ctx.enter_context(nc.Block())

        @block.sync
        def _(sp):
            def x_rows(b, ahead):
                return x[bass.ds(b + ahead, 1), :, :].rearrange("o (t p) e -> p (o t) e", p=P)

            sp.dma_start(wdq_st[:, 0, :], w_dq[0:P, :]).then_inc(ld_q, 16)
            sp.dma_start(wdq_st[0:CQ - P, 1, :], w_dq[P:CQ, :]).then_inc(ld_q, 16)
            sp.dma_start(wu_st[:, 0, :], wu_t[0:P, :]).then_inc(ld_q, 16)
            sp.dma_start(wu_st[0:CQ - P, 1, :], wu_t[P:CQ, :]).then_inc(ld_q, 16)
            sp.dma_start(idx_sb[:, :], chosen).then_inc(ld_idx, 16)
            sp.dma_start(xn[:, :, :], x_rows(0, 0)).then_inc(x_loaded.sem, 16)
            sp.dma_start(ct[:, :, :], c_t.rearrange("(c p) b -> p c b", p=P)).then_inc(ld_mod, 16)
            sp.dma_start(wmod_st, wmod.rearrange("(c p) n -> p c n", p=P)).then_inc(ld_mod, 16)
            sp.dma_start(wd_st, wdkv_t.rearrange("(c p) n -> p c n", p=P)).then_inc(ld_k, 16)
            sp.dma_start(gw_st, gw_t.rearrange("(c p) n -> p c n", p=P)).then_inc(ld_k, 16)
            for c in range(EC):
                sp.dma_start(wk_st[c], wk_t[c * P:(c + 1) * P, :]).then_inc(ld_k, 16)
            sp.dma_start(table[:, 0, :], cos_t).then_inc(ld_tab, 16)
            sp.dma_start(table[:, 1, :], sin_t).then_inc(ld_tab, 16)
            sp.dma_start(wuk[:, :], wuk_t).then_inc(ld_small, 16)
            sp.dma_start(wuv[:, :], wuv_t).then_inc(ld_small, 16)
            sp.dma_start(wo[:, :, :], wo_p.rearrange("g p e -> p g e")).then_inc(ld_small, 16)
            sp.dma_start(grp_i[0:NX, :], groups).then_inc(ld_small, 16)
            sp.dma_start(grp_i[NX:2 * NX, :], groups).then_inc(ld_small, 16)
            sp.wait_ge(ld_idx, 16)
            for g in range(G):
                xp = sp.value_load(idx_sb[0:1, g:g + 1], min_val=0, max_val=NX - 1)
                src = gup_t[bass.ds(xp, 1), :, :].rearrange("o (c p) (a i) -> p (o c) a i", p=P, a=2)
                for c in range(EC):
                    sp.dma_start(gu_st[c].rearrange("p (a g i) -> p g a i", a=2, g=G)[:, g, :, :], src[:, c, :, :])\
                      .then_inc(ld_ffn, 16)
                for row, n in DOWN_PIECES[g]:
                    r = row - g * FI
                    sp.dma_start(dn[row % P:row % P + n, row // P, :],
                                 dn_t[bass.ds(xp, 1), r:r + n, :].rearrange("o r e -> (o r) e")).then_inc(ld_ffn, 16)

            sp.wait_ge(gates_ready, 1)
            sp.dma_start(gates_dram, gates).then_inc(gates_stored, 16)
            sp.wait_ge(gates_stored, 16)
            sp.wait_ge(key_ones, 1)

            def program(sp, b, part, steps):
                for step in steps:
                    kind, ahead = step[0], step[1] if len(step) > 1 else 0
                    if kind == "heads":
                        g = step[2]
                        par = g % 2
                        wait_alone(sp, prob_filled, b, ahead, (g - 2) * NST + NST - 1)
                        for t, dst in ((0, kh), (1, qh)):
                            wait_alone(sp, rope_ready, b, ahead, 2 * g + t)
                            for half, slot in ((0, 0), (1, 2)):
                                sp.dma_start(dst[half * HALF:(half + 1) * HALF, par, :, :].bitcast(F32),
                                             rot[:, par, t, slot, :]).then_inc(heads_loaded[par].sem, 16)
                        row, pair = (g % 2) * HG * HD, g // 2
                        for t, dst in ((0, kh), (1, qh)):
                            wait_alone(sp, con_ready, b, ahead, 2 * pair + t)
                            sp.dma_start(dst[RD:DK, par, :, :].bitcast(F32), con[row:row + HG * HD, pair, t, :])\
                              .then_inc(heads_loaded[par].sem, 16)
                    elif kind == "shift":
                        g = step[2]
                        wait_alone(sp, nm_ready, b, ahead, g)
                        sp.dma_start(qh[DK:DK + 1, g % 2, :, :].bitcast(F32).rearrange("o h (q t) -> o h q t", q=TT),
                                     nm[:, g % 2, :]).then_inc(shift_loaded[g % 2].sem, 16)
                    elif kind == "loads":
                        wait_alone(sp, stored, b, ahead - 1, 0)
                        wait_alone(sp, down_gated, b, ahead - 1, 1)
                        sp.dma_start(xr[:, :, :], x_rows(b, ahead)).then_inc(res_loaded.sem, 16)
                        sp.dma_start(gate_bc[:, :], gates_dram[bass.ds(b + ahead, 1), :].broadcast_to([P, 2 * E]))\
                          .then_inc(gate_loaded.sem, 16)
                    elif kind == "load_next":
                        if isinstance(b, int) and b == 0:
                            wait_alone(sp, lo_ready[0], b, 0, 1)
                        else:
                            wait_alone(sp, lo_ready[1], b, -1, 1)
                        sp.dma_start(xn[:, :, :], x_rows(b, ahead)).then_inc(x_loaded.sem, 16)
                    elif kind == "store":
                        wait_alone(sp, down_added, b, ahead, 1)
                        sp.dma_start(out[bass.ds(b + ahead, 1), :, :].rearrange("o (t p) e -> p (o t) e", p=P),
                                     xr[:, :, :]).then_inc(stored.sem, 16)
            parts(program)(sp)
            sp.wait_ge(stored.sem, 16 * B)

        @block.gpsimd
        def _(pool):
            pool.memset(ident[:, :], 0.0).then_inc(pool_setup, 1)
            pool.memset(mask_qk[:, :], 0.0).then_inc(pool_setup, 1)
            pool.memset(mask_kq[:, :], 0.0).then_inc(pool_setup, 1)
            pool.memset(half_neg[:, :], -0.5)
            pool.memset(vals[:, :, :, :, :], 0.0).then_inc(pool_setup, 1)
            pool.wait_ge(pool_setup, 4)
            pool.memset(vals[:, :, 0, :, HD:HD + 1], 1.0)
            pool.memset(vals[:, :, 1, :, 0:1], 1.0)
            pool.affine_select(out=ident[:, :], in_=ident[:, :], compare_op=ALU.not_equal, fill=1.0, base=0,
                               pattern=[[-1, P]], channel_multiplier=1).then_inc(pool_setup, 1)
            pool.affine_select(out=mask_qk[:, :], in_=mask_qk[:, :], compare_op=ALU.is_ge, fill=MASKED, base=0,
                               pattern=[[-1, P]], channel_multiplier=1)
            pool.affine_select(out=mask_kq[:, :], in_=mask_kq[:, :], compare_op=ALU.is_ge, fill=MASKED, base=0,
                               pattern=[[1, P]], channel_multiplier=-1)
            pool.iota(gnum.rearrange("p (g i) -> p g i", g=G), pattern=[[1, G], [0, FI]], base=0,
                      channel_multiplier=0, allow_small_or_imprecise_dtypes=True).then_inc(pool_setup, 1)
            pool.wait_ge(pool_setup, 6)
            pool.tensor_copy(ident_b[:, :], ident[:, :]).then_inc(consts_ready, 1)

            def program(pool, b, part, steps):
                for step in steps:
                    kind, ahead = step[0], step[1] if len(step) > 1 else 0
                    if kind in ("norm1", "norm2"):
                        i = int(kind[-1]) - 1
                        wait(pool, var_ready[i], b, ahead, 0)
                        pool.tensor_tensor(rstd, veps, half_neg[:, :], ALU.pow).then_inc(rstd_ready[i].sem, 1)
                    elif kind == "rotate" and step[4] == 1:
                        g, t = step[2:4]
                        room = rot[:, g % 2, t, :, :]
                        wait(pool, rotated, b, ahead, 2 * g + t)
                        pool.tensor_tensor(room[:, 0, :], room[:, 0, :], room[:, 3, :], ALU.subtract)
                        pool.tensor_tensor(room[:, 2, :], room[:, 2, :], room[:, 1, :], ALU.add)\
                            .then_inc(rope_ready.sem, 1)
            parts(program)(pool)

        @block.scalar
        def _(sc):
            def program(sc, b, part, steps):
                for step in steps:
                    kind, ahead = step[0], step[1] if len(step) > 1 else 0
                    if kind == "silu":
                        sc.wait_ge(ld_mod, 32)
                        sc.activation(scT[:, :, :], ct[:, :, :], ACT.Tanh, scale=0.5).then_inc(tanh_c_ready, 1)
                    elif kind == "split_keys":
                        sc.wait_ge(ld_k, 64)
                        sc.activation(wd_hi[:, :, :], wd_st, ACT.Copy).then_inc(keys_hi_ready, 1)
                        for k in range(EC):
                            sc.activation(wk_hi[:, k, :], wk_st[k], ACT.Copy).then_inc(keys_hi_ready, 1)
                        sc.activation(gw_hi[:, :, :], gw_st, ACT.Copy).then_inc(keys_hi_ready, 1)
                    elif kind == "fuse":
                        i = step[1]
                        ps = wait_full(sc, b, part, step)
                        ec, c0, n = FUSE[i]
                        sc.activation(wq_hi[:, ec, c0:c0 + n], ps[:, 0:n], ACT.Copy).then_inc(fuse_hi_ready, 1)
                    elif kind == "split_ffn":
                        k = step[1]
                        sc.wait_ge(ld_ffn, 16 * (EC * G + sum(map(len, DOWN_PIECES))))
                        sc.activation(gu_hi[:, k, :], gu_st[k], ACT.Copy).then_inc(ffn_hi_ready, 1)
                    elif kind == "loads" and part == "body" and isinstance(b, int):
                        sc.wait_ge(ffn_split, EC)
                    elif kind in ("turn1", "turn2"):
                        i, c = int(kind[-1]) - 1, step[2]
                        if kind == "turn1" and part == "setup" and c == 0:
                            sc.wait_ge(mod_ready, 1)
                        if c == 0:
                            wait_full(sc, b, part, (kind, ahead, EC - 1))
                        ps = wait_full(sc, b, part, step)
                        sc.activation(hf[:, c, :], ps[:, :], ACT.Identity,
                                      scale=modT[:, 4 * i + 2 + c, bass.ds(b + ahead, 1)],
                                      bias=modT[:, 4 * i + c, bass.ds(b + ahead, 1)]).then_inc(turned[i].sem, 1)
                    elif kind == "latent":
                        wait(sc, vals_ready, b, ahead - 1, 1)
                        ps = wait_full(sc, b, part, step)
                        sc.activation(ckv[:, :], ps[0:CKV, :], ACT.Copy).then_inc(latent_ready.sem, 1)
                    elif kind == "values":
                        i = step[2]
                        wait(sc, value_added, b, ahead, -1)
                        if part == "setup" and i == 0:
                            sc.wait_ge(pool_setup, 5)
                        ps = wait_full(sc, b, part, step)
                        for parity in range(2):
                            last = sc.activation(vals[:, 2 * i:2 * i + 2, parity, :, parity * HD:(parity + 1) * HD],
                                                 ps[:, :].rearrange("p (t a k d) -> p t a k d", t=2, a=2, d=HD)
                                                 [:, :, parity, :, :], ACT.Copy)
                        last.then_inc(vals_ready.sem, 1)
                    elif kind == "content":
                        g = step[2]
                        wait_parity(sc, heads_loaded, b, ahead - 1, g - 3 + NG)
                        if part == "setup" and g == 2:
                            sc.wait_ge(spread_ready, 1)
                        for t in range(2):
                            ps = wait_full(sc, b, part, (*step, t))
                            sc.activation(con[:, g // 2, t, :], ps[:, :], ACT.Copy).then_inc(con_ready.sem, 1)
                    elif kind == "shift":
                        g = step[2]
                        par, back, k = head_value(b, ahead - 1, g - 2 + NG)
                        wait(sc, shift_loaded[par], b, back, k)
                        ps = wait_full(sc, b, part, step)
                        sc.activation(nm[:, g % 2, :], ps[0:HG * TT, 0:P], ACT.Copy, scale=-1.0)\
                          .then_inc(nm_ready.sem, 1)
                    elif kind == "score":
                        g, n = step[2:]
                        u, h0, nh = ST_JOBS[n]
                        w = ST_TILES[u][2]
                        at, cols = (u % PT_RING) * PT_COLS + h0 * w, nh * w
                        wait(sc, value_added, b, ahead, g * NTILE + u - PT_RING)
                        wait(sc, prob_filled, b, ahead, g * NST + n)
                        sc.activation(pt[:, at:at + cols], prob[(g * NST + n) % PROB_RING][:, 0:cols], ACT.Exp,
                                      scale=SCALE).then_inc(exp_ready.sem, 1)
                    elif kind == "top":
                        wait(sc, logits_shifted, b, ahead, 0)
                        sc.activation(ex[:, :, :], lg[:, :, :], ACT.Exp).then_inc(top_exp.sem, 1)
                    elif kind == "turn_w":
                        ps = wait_full(sc, b, part, step)
                        sc.activation(wT[0:NX, :], ps[0:NX, :], ACT.Copy).then_inc(wT_hi_ready.sem, 1)
                    elif kind == "gate":
                        k = step[2]
                        if k >= INNER_RING:
                            wait(sc, down_done, b, ahead, k - INNER_RING)
                        ps = wait_full(sc, b, part, step)
                        sc.activation(inner[:, k % INNER_RING, :], ps[:, :], ACT.Tanh, scale=0.5).then_inc(tanh_ready.sem, 1)
            parts(program)(sc)

        @block.vector
        def _(ve):
            chained = [0]

            def chain(instruction):
                chained[0] += 1
                instruction.then_inc(setup_chain, 1)
                ve.wait_ge(setup_chain, chained[0])

            for parity in range(2):
                chain(ve.memset(keep[:, parity:parity + 1], float(parity)))
                for q in range(0, P, HV):
                    last = ve.memset(keep[q:q + HD, parity:parity + 1], 1.0 - parity)
            chain(last)
            ve.memset(kh[64:P, :, :, :].bitcast(F32), 1.0)
            ve.memset(qh[64:P, :, :, :].bitcast(F32), 0.0).then_inc(key_ones, 1)

            def program(ve, b, part, steps):
                for step in steps:
                    kind, ahead = step[0], step[1] if len(step) > 1 else 0
                    if kind == "silu":
                        ve.wait_ge(tanh_c_ready, 1)
                        chain(ve.scalar_tensor_tensor(scT[:, :, :], scT[:, :, :], 1.0, ct[:, :, :], ALU.add, ALU.mult))
                        ve.tensor_scalar(scT[:, :, :], scT[:, :, :], 0.5, None, ALU.mult).then_inc(silu_ready, 1)
                    elif kind == "split_keys":
                        ve.wait_ge(keys_hi_ready, 2 + EC)
                        ve.tensor_tensor(wd_lo[:, :, :], wd_st, wd_hi[:, :, :], ALU.subtract)
                        for k in range(EC):
                            ve.tensor_tensor(wk_lo[:, k, :], wk_st[k], wk_hi[:, k, :], ALU.subtract)
                        ve.tensor_tensor(gw_lo[:, :, :], gw_st, gw_hi[:, :, :], ALU.subtract).then_inc(keys_split, 1)
                    elif kind == "mod":
                        ps = wait_full(ve, b, part, step)
                        v = ps[:, 0:8 * B].rearrange("p (c b) -> p c b", b=B)
                        chain(ve.tensor_copy(modT[:, :, :], v))
                        ve.sem_inc(mod_read, 1)
                        for c in (2, 6):
                            last = ve.tensor_scalar(modT[:, c:c + 2, :], modT[:, c:c + 2, :], 1.0, None, ALU.add)
                        last.then_inc(mod_ready, 1)
                    elif kind == "gates":
                        ps = wait_full(ve, b, part, step)
                        ve.tensor_scalar(gates, ps[0:B, :], 0.0, 2.0, ALU.is_ge, ALU.mult)
                        chain(ve.tensor_copy(gates_abs, ps[0:B, :]))
                        ve.sem_inc(gates_read, 1)
                        chain(ve.scalar_tensor_tensor(gates_abs, gates_abs, -1.0, gates_abs,
                                                      ALU.mult, ALU.max))
                        chain(ve.tensor_scalar(gates_abs, gates_abs, 0.25, None, ALU.max))
                        ve.scalar_tensor_tensor(gates, gates, -1.0, gates_abs,
                                                ALU.add, ALU.mult).then_inc(gates_ready, 1)
                    elif kind == "spread":
                        ve.wait_ge(ld_small, 16 * 5)
                        ve.wait_ge(pool_setup, 6)
                        chain(ve.tensor_copy(gid, grp_i[:, :]))
                        ve.tensor_scalar(spread[:, :], gnum[0:2 * NX, :], gid, None, ALU.is_equal)\
                          .then_inc(spread_ready, 1)
                    elif kind == "fuse":
                        i = step[1]
                        ps = wait_full(ve, b, part, step)
                        ec, c0, n = FUSE[i]
                        ve.wait_ge(fuse_hi_ready, i + 1)
                        ve.tensor_tensor(wq_lo[:, ec, c0:c0 + n], ps[:, 0:n], wq_hi[:, ec, c0:c0 + n],
                                         ALU.subtract).then_inc(fuse_read, 1)
                    elif kind == "split_ffn":
                        k = step[1]
                        ve.wait_ge(ffn_hi_ready, k + 1)
                        ve.tensor_tensor(gu_lo[:, k, :], gu_st[k], gu_hi[:, k, :], ALU.subtract).then_inc(ffn_split, 1)
                    elif kind in ("stats1", "stats2"):
                        i = int(kind[-1]) - 1
                        if i == 0:
                            wait_alone(ve, x_loaded, b, ahead, 0)
                            for t in range(TT):
                                last = ve.bn_stats(stat[:, t, :], xn[:, t, :])
                            last.then_inc(stats_read[i].sem, 1)
                        wait_alone(ve, stats_read[i], b, ahead, 0)
                        for t in range(TT):
                            last = ve.bn_aggr(mv[:, t, :], stat[:, t, :])
                        last.then_inc(aggregated[i].sem, 1)
                        wait(ve, aggregated[i], b, ahead, 0)
                        ve.tensor_scalar(veps, mv[:, :, 1], EPS, None, ALU.add).then_inc(var_ready[i].sem, 1)
                    elif kind in ("norm1", "norm2"):
                        i = int(kind[-1]) - 1
                        src = xr if i else xn
                        wait(ve, rstd_ready[i], b, ahead, 0)
                        for t in range(TT):
                            last = ve.tensor_scalar(xn[:, t, :], src[:, t, :], mv[:, t, 0:1], rstd[:, t:t + 1],
                                                    ALU.subtract, ALU.mult)
                        last.then_inc(normed[i].sem, 1)
                    elif kind in ("turn1", "turn2"):
                        i, c = int(kind[-1]) - 1, step[2]
                        hi, lo = ((h1_hi, h1_lo), (h2_hi, h2_lo))[i]
                        wait(ve, turned[i], b, ahead, c)
                        ve.tensor_copy(hi[:, c, :], hf[:, c, :]).then_inc(hi_ready[i].sem, 1)
                        wait(ve, hi_ready[i], b, ahead, c)
                        ve.tensor_tensor(lo[:, c, :], hf[:, c, :], hi[:, c, :], ALU.subtract)\
                          .then_inc(lo_ready[i].sem, 1)
                    elif kind == "rotate":
                        g, t, half = step[2:]
                        if part == "setup" and (g, t) == (0, 0):
                            ve.wait_ge(ld_tab, 32)
                        if half == 0:
                            wait_parity(ve, heads_loaded, b, ahead - 1, g - 2 + NG)
                        ps = wait_full(ve, b, part, ("rope", ahead, g, t, half))
                        last = ve.tensor_tensor(rot[:, g % 2, t, 2 * half:2 * half + 2, :],
                                                ps[:, :].unsqueeze(1).broadcast_to([P, 2, S]), table[:, :, :], ALU.mult)
                        if half == 1:
                            last.then_inc(rotated.sem, 1)
                    elif kind == "maxima":
                        g, i = step[2:]
                        ps = wait_full(ve, b, part, step)
                        if i == 0:
                            wait(ve, nm_ready, b, ahead, g - 2)
                        at = 0
                        pieces = MAX_JOBS[i]
                        if len(pieces) == 2 and pieces[0][1] == pieces[1][1]:
                            (h, q), w = pieces[0], (pieces[0][1] + 1) * P
                            dst = mcol[:, g % 2, :].rearrange("p (h q) -> p q h", h=HG)[:, q, h:h + 2]
                            last = ve.reduce_max(dst, ps[:, 0:2 * w].rearrange("p (h k) -> p h k", h=2), AX_X)
                        else:
                            for h, q in pieces:
                                w = (q + 1) * P
                                last = ve.reduce_max(mcol[:, g % 2, h * TT + q:h * TT + q + 1], ps[:, at:at + w], AX_X)
                                at += w
                        last.then_inc(max_read.sem, 1)
                    elif kind == "attn_out":
                        g, half = step[2:]
                        cols = slice(half * S // 2, (half + 1) * S // 2)
                        o, sums, k = ot[half][:, 0:S // 2], norm[:, cols], 2 * g + half
                        last_tile = [u for u in range(NTILE) if ST_TILES[u][1] < cols.stop][-1]
                        wait_alone(ve, value_added, b, ahead, g * NTILE + last_tile)
                        if g % 2:
                            wait_alone(ve, normalised, b, ahead, k - 2)
                        else:
                            wait_alone(ve, pair_ready, b, ahead, 2 * (g // 2 - 1) + half)
                        ve.stream_shuffle(sums, o, [(1 - g % 2) * HD] * 32).then_inc(sums_moved.sem, 1)
                        wait(ve, sums_moved, b, ahead, k)
                        ve.reciprocal(sums, sums).then_inc(sums_inverted.sem, 1)
                        wait(ve, sums_inverted, b, ahead, k)
                        pair = on[:, g // 2, cols]
                        ve.scalar_tensor_tensor(sums if g % 2 else pair, o, keep[:, g % 2:g % 2 + 1], sums,
                                                ALU.mult, ALU.mult).then_inc(normalised.sem, 1)
                        if g % 2:
                            wait(ve, normalised, b, ahead, k)
                            ve.tensor_tensor(pair, pair, sums, ALU.add).then_inc(pair_ready.sem, 1)
                    elif kind == "mix":
                        i = step[2]
                        if i == 0:
                            wait(ve, gate_loaded, b, ahead, 0)
                            wait(ve, res_loaded, b, ahead, 0)
                        wait(ve, mix_filled, b, ahead, i)
                        ps = ot[i]
                        gate = gate_bc[:, 0:E].unsqueeze(1).broadcast_to([P, 2, E])
                        ve.tensor_tensor(sum2[:, :, :], ps[:, :].rearrange("p (t e) -> p t e", t=2), gate, ALU.mult)\
                          .then_inc(mix_gated.sem, 1)
                        wait(ve, mix_gated, b, ahead, i)
                        ve.tensor_tensor(xr[:, 2 * i:2 * i + 2, :], xr[:, 2 * i:2 * i + 2, :], sum2[:, :, :], ALU.add)\
                          .then_inc(mix_added.sem, 1)
                        wait_alone(ve, mix_added, b, ahead, i)
                        for t in (2 * i, 2 * i + 1):
                            last = ve.bn_stats(stat[:, t, :], xr[:, t, :])
                        if i == 1:
                            last.then_inc(stats_read[1].sem, 1)
                    elif kind == "logits":
                        i = step[2]
                        ps = wait_full(ve, b, part, step)
                        ve.tensor_copy(lg[:, 2 * i:2 * i + 2, :], ps[:, 0:2 * NX].rearrange("p (t n) -> p t n", t=2))\
                          .then_inc(logits_read.sem, 1)
                    elif kind == "top":
                        bc = lambda v: v.unsqueeze(2).broadcast_to([P, TT, NX])
                        wait(ve, logits_read, b, ahead, 1)
                        ve.reduce_max(mx, lg[:, :, :], AX_X).then_inc(row_max.sem, 1)
                        wait(ve, row_max, b, ahead, 0)
                        ve.tensor_tensor(lg[:, :, :], lg[:, :, :], bc(mx), ALU.subtract).then_inc(logits_shifted.sem, 1)
                        wait_alone(ve, top_exp, b, ahead, 0)
                        for t in range(TT):
                            last = ve.max(top8[:, t, :], ex[:, t, :])
                        last.then_inc(top_found.sem, 1)
                        wait_alone(ve, top_found, b, ahead, 0)
                        for t in range(TT):
                            last = ve.match_replace(rest[:, t, :], top8[:, t, :], ex[:, t, :], -1.0)
                        last.then_inc(top_removed.sem, 1)
                        ve.reduce_sum(den, top8, AX_X).then_inc(top_summed.sem, 1)
                        wait(ve, top_summed, b, ahead, 0)
                        ve.reciprocal(rden, den).then_inc(sum_inverted.sem, 1)
                        wait(ve, top_removed, b, ahead, 0)
                        ve.scalar_tensor_tensor(rest[:, :, :], rest[:, :, :], 0.0, ex[:, :, :], ALU.is_lt, ALU.mult)\
                          .then_inc(top_kept.sem, 1)
                        wait(ve, top_kept, b, ahead, 0)
                        wait(ve, sum_inverted, b, ahead, 0)
                        ve.tensor_tensor(rest[:, :, :], rest[:, :, :], bc(rden), ALU.mult)\
                          .then_inc(weights_ready.sem, 1)
                    elif kind == "turn_w":
                        ps = wait_full(ve, b, part, step)
                        wait(ve, wT_hi_ready, b, ahead, 0)
                        ve.tensor_tensor(wT[NX:2 * NX, :], ps[0:NX, :], wT[0:NX, :], ALU.subtract)\
                          .then_inc(wT_lo_ready.sem, 1)
                    elif kind == "gate":
                        k = step[2]
                        wait(ve, tanh_ready, b, ahead, k)
                        ps, room = bank(part, PLACES[part][0][step]), inner[:, k % INNER_RING, :]
                        ve.scalar_tensor_tensor(room, room, 1.0, ps[:, :], ALU.add, ALU.mult)\
                          .then_inc(gate_used.sem, 1)
                    elif kind == "up":
                        k = step[2]
                        wait(ve, gate_used, b, ahead, k)
                        ps = wait_full(ve, b, part, step)
                        room = inner[:, k % INNER_RING, :]
                        ve.scalar_tensor_tensor(room, room, 0.5, ps[:, :], ALU.mult, ALU.mult)\
                          .then_inc(up_used.sem, 1)
                    elif kind == "weigh":
                        k = step[2]
                        wait(ve, up_used, b, ahead, k)
                        ps = wait_full(ve, b, part, step)
                        room = inner[:, k % INNER_RING, :]
                        ve.tensor_tensor(room, room, ps[:, :], ALU.mult).then_inc(inner_ready.sem, 1)
                    elif kind == "join":
                        i = step[2]
                        wait(ve, down_done, b, ahead, FT - 1)
                        ps = ot[i]
                        gate = gate_bc[:, E:2 * E].unsqueeze(1).broadcast_to([P, 2, E])
                        ve.tensor_tensor(sum2[:, :, :], ps[:, :].rearrange("p (t e) -> p t e", t=2), gate, ALU.mult)\
                          .then_inc(down_gated.sem, 1)
                        wait(ve, down_gated, b, ahead, i)
                        ve.tensor_tensor(xr[:, 2 * i:2 * i + 2, :], xr[:, 2 * i:2 * i + 2, :], sum2[:, :, :], ALU.add)\
                          .then_inc(down_added.sem, 1)
                        wait(ve, down_added, b, ahead, i)
            parts(program)(ve)

        @block.tensor
        def _(pe):
            def three(ps, whi, wlo, xhi, xlo, ready=lambda c: None):
                for c in range(EC):
                    ready(c)
                    pe.matmul(ps, wlo(c), xhi(c), start=c == 0, stop=False)
                    pe.matmul(ps, whi(c), xlo(c), start=False, stop=False)
                    last = pe.matmul(ps, whi(c), xhi(c), start=False, stop=c == EC - 1)
                return last

            def columns(hi, lo, c0, n):
                return (lambda c: hi[:, c, c0:c0 + n]), (lambda c: lo[:, c, c0:c0 + n])

            rows1 = (lambda c: h1_hi[:, c, :]), (lambda c: h1_lo[:, c, :])
            rows2 = (lambda c: h2_hi[:, c, :]), (lambda c: h2_lo[:, c, :])

            def program(pe, b, part, steps):
                for step in steps:
                    kind, ahead = step[0], step[1] if len(step) > 1 else 0
                    if kind == "mod":
                        pe.wait_ge(silu_ready, 1)
                        ps = take_bank(pe, b, part, step)
                        n = 0
                        for which in (0, 1, 3, 4):
                            for c in range(EC):
                                for k in range(EC):
                                    at = which * E + c * P
                                    last = pe.matmul(ps[:, n * B:(n + 1) * B], wmod_st[:, k, at:at + P], scT[:, k, :],
                                                     start=k == 0, stop=k == EC - 1)
                                n += 1
                        last.then_inc(full_sem, 1)
                    elif kind == "gates":
                        ps = take_bank(pe, b, part, step)
                        for i, which in enumerate((2, 5)):
                            for k in range(EC):
                                last = pe.matmul(ps[0:B, i * E:(i + 1) * E], scT[:, k, :],
                                                 wmod_st[:, k, which * E:(which + 1) * E], start=k == 0, stop=k == EC - 1)
                        last.then_inc(full_sem, 1)
                    elif kind == "fuse":
                        if step[1] == 0:
                            pe.wait_ge(ld_q, 64)
                        ps = take_bank(pe, b, part, step)
                        ec, c0, n = FUSE[step[1]]
                        pe.matmul(ps[:, 0:n], wdq_st[:, 0, ec * P:(ec + 1) * P], wu_st[:, 0, c0:c0 + n],
                                  start=True, stop=False)
                        pe.matmul(ps[:, 0:n], wdq_st[0:CQ - P, 1, ec * P:(ec + 1) * P], wu_st[0:CQ - P, 1, c0:c0 + n],
                                  start=False, stop=True).then_inc(full_sem, 1)
                    elif kind in ("turn1", "turn2"):
                        i, c = int(kind[-1]) - 1, step[2]
                        if part == "setup" and c == 0:
                            pe.wait_ge(consts_ready, 1)
                        wait(pe, normed[i], b, ahead, 0)
                        ps = take_bank(pe, b, part, step)
                        for t in range(TT):
                            last = pe.transpose(ps[:, t * P:(t + 1) * P], xn[:, t, c * P:(c + 1) * P], ident[:, :])
                        last.then_inc(full_sem, 1)
                    elif kind == "latent":
                        if part == "setup":
                            pe.wait_ge(keys_split, 1)
                            pe.wait_ge(ld_small, 16 * 5)
                        ps = take_bank(pe, b, part, step)
                        three(ps[0:CKV, :], *columns(wd_hi, wd_lo, 0, CKV), *rows1,
                              ready=lambda c: wait(pe, lo_ready[0], b, ahead, c)).then_inc(full_sem, 1)
                    elif kind == "rope":
                        g, t = step[2:]
                        hi, lo = ((wk_hi, wk_lo), (wq_hi, wq_lo))[t]
                        if part == "setup" and t == 1:
                            pe.wait_ge(fuse_read, len(FUSE))
                        for half in range(2):
                            ps = take_bank(pe, b, part, (*step, half))
                            three(ps[:, :], *columns(hi, lo, g * NROPE + half * P, P), *rows1).then_inc(full_sem, 1)
                    elif kind == "content":
                        g = step[2]
                        wait(pe, latent_ready, b, ahead, 0)
                        ps = take_bank(pe, b, part, (*step, 0))
                        pe.matmul(ps[:, :], wuk[:, g * HG * HD:(g + 2) * HG * HD], ckv[:, :], start=True, stop=True)\
                          .then_inc(full_sem, 1)
                        ps = take_bank(pe, b, part, (*step, 1))
                        three(ps[:, :], *columns(wq_hi, wq_lo, NG * NROPE + g * HG * HD, P), *rows1)\
                            .then_inc(full_sem, 1)
                    elif kind == "values":
                        i = step[2]
                        ps = take_bank(pe, b, part, step)
                        for t in range(2):
                            tok = (2 * i + t) * P
                            last = pe.matmul(ps[:, t * E:(t + 1) * E], ckv[:, tok:tok + P], wuv[:, :],
                                             start=True, stop=True)
                        last.then_inc(full_sem, 1)
                    elif kind == "maxima":
                        g, i = step[2:]
                        if i == 0:
                            wait_parity(pe, heads_loaded, b, ahead, g)
                        ps = take_bank(pe, b, part, step)
                        at, par, ends = 0, g % 2, []
                        for h, q in MAX_JOBS[i]:
                            w = (q + 1) * P
                            pe.matmul(ps[:, at:at + w], qh[0:DK, par, h, q * P:(q + 1) * P], kh[0:DK, par, h, 0:w],
                                      start=at == 0, stop=False)
                            at += w
                            ends.append(at)
                        n, apart = len(ends), ends[-1] - ends[0] or P
                        own = ps[:, at - n * apart:at].rearrange("p (n k) -> p n k", n=n)[:, :, apart - P:apart]
                        last = pe.matmul(own, ident_b[:, :], mask_qk[:, :].unsqueeze(1).broadcast_to([P, n, P]),
                                         start=False, stop=True)
                        last.then_inc(full_sem, 1)
                    elif kind == "shift":
                        g = step[2]
                        wait(pe, max_read, b, ahead, g * NMAX + NMAX - 1)
                        ps = take_bank(pe, b, part, step)
                        pe.transpose(ps[0:HG * TT, 0:P], mcol[:, g % 2, :], ident[:, :]).then_inc(full_sem, 1)
                    elif kind == "score":
                        g, n = step[2:]
                        u, h0, nh = ST_JOBS[n]
                        j, q0, w, diagonal = ST_TILES[u]
                        par = g % 2
                        if n == 0:
                            wait_parity(pe, shift_loaded, b, ahead, g)
                        ps = prob[(g * NST + n) % PROB_RING]
                        wait(pe, exp_ready, b, ahead, g * NST + n - PROB_RING)
                        for i in range(nh):
                            h, at, keys = h0 + i, i * w, slice(j * P, (j + 1) * P)
                            last = pe.matmul(ps[:, at:at + w], kh[:, par, h, keys].bitcast(F32),
                                             qh[:, par, h, q0:q0 + w].bitcast(F32),
                                             start=i == 0, stop=i == nh - 1 and not diagonal)
                        if diagonal:
                            last = pe.matmul(ps[:, 0:nh * w].rearrange("p (h q) -> p h q", h=nh)[:, :, 0:P], ident_b[:, :],
                                             mask_kq[:, :].unsqueeze(1).broadcast_to([P, nh, P]), start=False, stop=True)
                        last.then_inc(prob_sem, 1)
                    elif kind == "value":
                        g, u = step[2:]
                        j, q0, w, _ = ST_TILES[u]
                        half = q0 // (S // 2)
                        if u == 0:
                            wait(pe, vals_ready, b, ahead, 1)
                        if j == 0:
                            if g > 0:
                                wait(pe, normalised, b, ahead, 2 * (g - 1) + half)
                            else:
                                wait(pe, down_gated, b, ahead - 1, half)
                        jobs = [n for n in range(NST) if ST_JOBS[n][0] == u]
                        wait(pe, exp_ready, b, ahead, g * NST + jobs[-1])
                        o, c0 = ot[half], q0 - half * S // 2
                        final = u == NTILE - 1 or ST_TILES[u + 1][0] == 0
                        for h in range(HG):
                            at, k = (u % PT_RING) * PT_COLS + h * w, (g // 2) * HG + h
                            last = pe.matmul(o[HV * h:HV * (h + 1), c0:c0 + w], vals[:, j, g % 2, k, :],
                                             pt[:, at:at + w], start=j == 0, stop=final)
                        last.then_inc(value_added.sem, 1)
                    elif kind == "mix":
                        i = step[2]
                        for t in range(2):
                            tok = (2 * i + t) * P
                            for pair in range(NPAIR):
                                if (t, pair) == (0, 0):
                                    wait(pe, pair_ready, b, ahead, 2 * (NPAIR - 1) + i)
                                last = pe.matmul(ot[i][:, t * E:(t + 1) * E], on[:, pair, tok:tok + P], wo[:, pair, :],
                                                 start=pair == 0, stop=pair == NPAIR - 1)
                        last.then_inc(mix_filled.sem, 1)
                    elif kind == "logits":
                        i = step[2]
                        ps = take_bank(pe, b, part, step)
                        for t in range(2):
                            tok = (2 * i + t) * P
                            last = three(ps[:, t * NX:(t + 1) * NX],
                                         lambda c: h2_hi[:, c, tok:tok + P], lambda c: h2_lo[:, c, tok:tok + P],
                                         lambda c: gw_hi[:, c, :], lambda c: gw_lo[:, c, :],
                                         ready=lambda c: wait(pe, lo_ready[1], b, ahead, c))
                        last.then_inc(full_sem, 1)
                    elif kind in ("gate", "up"):
                        k = step[2]
                        if isinstance(b, int) and b == 0 and kind == "gate" and k == 0:
                            pe.wait_ge(ffn_split, EC)
                        ps = take_bank(pe, b, part, step)
                        at = (kind == "up") * G * FI + k * P
                        three(ps[:, :], *columns(gu_hi, gu_lo, at, P), *rows2).then_inc(full_sem, 1)
                    elif kind == "turn_w":
                        wait(pe, weights_ready, b, ahead, 0)
                        ps = take_bank(pe, b, part, step)
                        for t in range(TT):
                            last = pe.transpose(ps[0:NX, t * P:(t + 1) * P], rest[:, t, :], ident[:, :])
                        last.then_inc(full_sem, 1)
                    elif kind == "weigh":
                        k = step[2]
                        wait(pe, wT_lo_ready, b, ahead, 0)
                        if isinstance(b, int) and b == 0 and k == 0:
                            pe.wait_ge(spread_ready, 1)
                        ps = take_bank(pe, b, part, step)
                        pe.matmul(ps[:, :], spread[:, k * P:(k + 1) * P], wT[:, :], start=True, stop=True)\
                          .then_inc(full_sem, 1)
                    elif kind == "down":
                        k = step[2]
                        if k == 0:
                            wait(pe, mix_gated, b, ahead, 1)
                        wait(pe, inner_ready, b, ahead, k)
                        for t in range(TT):
                            last = pe.matmul(ot[t // 2][:, (t % 2) * E:(t % 2 + 1) * E],
                                             inner[:, k % INNER_RING, t * P:(t + 1) * P], dn[:, k, :],
                                             start=k == 0 and t % 2 == 0, stop=k == FT - 1 and t % 2 == 1)
                        last.then_inc(down_done.sem, 1)
            parts(program)(pe)


_OUT = (B, S, E)


def kernel(L0_attn_x, L0_attn_w_dq, L0_attn_w_uq, L0_attn_w_dkv, L0_attn_w_uk, L0_attn_w_uv, L0_attn_w_qr,
           L0_attn_w_kr, L0_attn_w_out, L0_ffn_gate_weight, L0_ffn_gate_up_proj, L0_ffn_down_proj,
           L0_ffn_merge_groups, L0_ffn_dominant_experts, L0_c, L0_wmod):
    import concourse.bacc as bacc
    from concourse.bass_utils import run_bass_kernel_spmd

    def rope_rows(w):
        w = np.asarray(w)
        return w.reshape(NG, HG, 2, HALF, w.shape[1]).transpose(0, 2, 3, 1, 4).reshape(NG * NROPE, w.shape[1])

    def content_rows(w):
        w = np.asarray(w)
        return w.reshape(NG, HG, HD, w.shape[1]).transpose(0, 2, 1, 3).reshape(H * HD, w.shape[1])

    inv_freq = (1.0 / 10000.0 ** (np.arange(0, RD, 2, dtype=np.float32) / np.float32(RD))).astype(np.float32)
    angle = inv_freq[:, None] * np.arange(S, dtype=np.float32)[None, :]
    wo = np.asarray(L0_attn_w_out).T.reshape(NPAIR, 2, HG, HD, E).transpose(0, 2, 1, 3, 4)
    wuv = np.asarray(L0_attn_w_uv).reshape(NPAIR, 2, HG, HD, CKV).transpose(1, 0, 2, 3, 4)
    data = {
        "x": np.asarray(L0_attn_x),
        "wu_t": np.concatenate([rope_rows(L0_attn_w_qr), content_rows(L0_attn_w_uq)]).T,
        "w_dq": np.asarray(L0_attn_w_dq),
        "wk_t": rope_rows(L0_attn_w_kr).T,
        "wdkv_t": np.asarray(L0_attn_w_dkv).T,
        "wuk_t": content_rows(L0_attn_w_uk).T,
        "wuv_t": wuv.reshape(H * HD, CKV).T,
        "wo_p": wo.reshape(NPAIR, P, E),
        "gw_t": np.asarray(L0_ffn_gate_weight).T,
        "gup_t": np.asarray(L0_ffn_gate_up_proj).transpose(0, 2, 1),
        "dn_t": np.asarray(L0_ffn_down_proj).transpose(0, 2, 1),
        "groups": np.asarray(L0_ffn_merge_groups).reshape(NX, 1),
        "chosen": np.asarray(L0_ffn_dominant_experts).reshape(1, G),
        "c_t": np.asarray(L0_c).T,
        "wmod": np.asarray(L0_wmod),
        "cos_t": np.repeat(np.cos(angle), HG, axis=0),
        "sin_t": np.repeat(np.sin(angle), HG, axis=0),
    }
    nc = bacc.Bacc("TRN2", target_bir_lowering=False, num_devices=1)
    arrays, args = {}, []
    for name, a in data.items():
        a = np.ascontiguousarray(a)
        arrays[f"{name}_dram"] = a
        args.append(nc.dram_tensor(f"{name}_dram", a.shape, mybir.dt.from_np(a.dtype), kind="ExternalInput").ap())
    out = nc.dram_tensor("out_dram", _OUT, F32, kind="ExternalOutput").ap()
    block_program(nc, *args, out)
    r = run_bass_kernel_spmd(nc, [arrays], core_ids=[0])
    return r.results[0]["out_dram"]
```
